# Optimizing a Trainium2 kernel written in Bass

```python
import numpy as np
import jax
import jax.numpy as jnp

def _softmax(x, axis=-1):
    return jax.nn.softmax(x, axis=axis)

def _gelu(x):
    return jax.nn.gelu(x, approximate=True)

def _silu(x):
    return jax.nn.silu(x)

def _sigmoid(x):
    return jax.nn.sigmoid(x)

def _layernorm(x, axis=-1, eps=1e-05):
    m = jnp.mean(x, axis=axis, keepdims=True)
    v = jnp.var(x, axis=axis, keepdims=True)
    return (x - m) / jnp.sqrt(v + eps)

def _scatter_add(tgt, idx, src, axis=0):
    return tgt.at[idx].add(src)

def _segment_sum(src, seg, n):
    return jax.ops.segment_sum(src, seg, n)
kernel_name = 'mk_adaln_d1_jaxref_r8_272dc4'

def setup_inputs(seed: int=0):
    np.random.seed(seed)
    _w = jnp.asarray

    def _L0_attn_setup():
        import jax, jax.numpy as jnp
        import numpy as np
        B, T, D = (2, 128, 256)
        H, DK, DV = (32, 48, 96)
        KD, VD = (H * DK, H * DV)
        CS = 4
        INTER = 704
        EPS = 1e-05

        def rmsnorm(x, w, eps=EPS):
            return x * jax.lax.rsqrt(jnp.mean(x * x, axis=-1, keepdims=True) + eps) * w

        def short_conv(x, w):
            K = w.shape[1]
            xp = jnp.pad(x, ((0, 0), (K - 1, 0), (0, 0)))
            out = sum((xp[:, k:k + x.shape[1], :] * w[:, k] for k in range(K)))
            return jax.nn.silu(out)

        def l2norm(x, eps=1e-06):
            return x * jax.lax.rsqrt(jnp.sum(x * x, axis=-1, keepdims=True) + eps)

        def gated_delta_rule(q, k, v, g, beta):
            scale = q.shape[-1] ** (-0.5)

            def step(S, inp):
                qt, kt, vt, gt, bt = inp
                S = S * jnp.exp(gt)[..., None, None]
                mem = jnp.einsum('bhk,bhkv->bhv', kt, S)
                delta = (vt - mem) * bt[..., None]
                S = S + jnp.einsum('bhk,bhv->bhkv', kt, delta)
                o = jnp.einsum('bhk,bhkv->bhv', qt * scale, S)
                return (S, o)
            S0 = jnp.zeros((q.shape[0], q.shape[2], q.shape[3], v.shape[3]), q.dtype)
            xs = (q.transpose(1, 0, 2, 3), k.transpose(1, 0, 2, 3), v.transpose(1, 0, 2, 3), g.transpose(1, 0, 2), beta.transpose(1, 0, 2))
            _, o = jax.lax.scan(step, S0, xs)
            return o.transpose(1, 0, 2, 3)
        key = jax.random.key(seed)
        ks = jax.random.split(key, 20)
        f = lambda k, sh, sc=0.02: jax.random.normal(k, sh, dtype=jnp.float32) * sc
        dt = jax.random.uniform(ks[7], (H,), minval=0.001, maxval=0.1)
        return dict(x=jax.random.normal(ks[0], (B, T, D), dtype=jnp.float32), rms1_w=jnp.ones((D,), jnp.float32), rms2_w=jnp.ones((D,), jnp.float32), Wq=f(ks[1], (D, KD)), Wk=f(ks[2], (D, KD)), Wv=f(ks[3], (D, VD)), Wa=f(ks[4], (D, H)), Wb=f(ks[5], (D, H)), Wg=f(ks[6], (D, VD)), dt_bias=jnp.log(jnp.expm1(dt)), A_log=jnp.log(jax.random.uniform(ks[8], (H,), minval=1.0, maxval=16.0)), conv_q_w=f(ks[9], (KD, CS), 0.5), conv_k_w=f(ks[10], (KD, CS), 0.5), conv_v_w=f(ks[11], (VD, CS), 0.5), gnorm_w=jnp.ones((DV,), jnp.float32), Wo=f(ks[12], (VD, D)), W1=f(ks[13], (D, INTER)), W3=f(ks[14], (D, INTER)), W2=f(ks[15], (INTER, D)))
    _L0_attn_in = _L0_attn_setup()

    def _L0_ffn_setup():
        import jax, jax.numpy as jnp
        import numpy as np
        K = 2

        def gelu(v):
            return jax.nn.gelu(v, approximate=False)
        key = jax.random.key(seed)
        ks = jax.random.split(key, 10)
        B, S, D, H, E = (4, 256, 256, 128, 8)
        SH = 2 * H
        u = lambda k_, shape, b: jax.random.uniform(k_, shape, jnp.float32, -b, b)
        return {'x': jax.random.normal(ks[0], (B, S, D), jnp.float32), 'gate_w': u(ks[1], (D, E), 1.0 / D), 'w1': u(ks[2], (E, D, H), 1.0 / D), 'b1': u(ks[3], (E, H), 1.0 / np.sqrt(D)), 'w2': u(ks[4], (E, H, D), 1.0 / H), 'b2': u(ks[5], (E, D), 1.0 / np.sqrt(H)), 'shared_w1': u(ks[6], (D, SH), 1.0 / D), 'shared_b1': u(ks[7], (SH,), 1.0 / np.sqrt(D)), 'shared_w2': u(ks[8], (SH, D), 1.0 / SH), 'shared_b2': u(ks[9], (D,), 1.0 / np.sqrt(SH))}
    _L0_ffn_in = _L0_ffn_setup()
    _L0_c = _w((lambda *s: np.random.randn(*s).astype(np.float32) * 0.05)(8, 256))
    _L0_wmod = _w((lambda *s: np.random.randn(*s).astype(np.float32) * 0.05)(256, 6 * 256) * 256 ** (-0.5))
    _d = {'L0_attn_x': _L0_attn_in['x'], 'L0_attn_rms1_w': _L0_attn_in['rms1_w'], 'L0_attn_rms2_w': _L0_attn_in['rms2_w'], 'L0_attn_Wq': _L0_attn_in['Wq'], 'L0_attn_Wk': _L0_attn_in['Wk'], 'L0_attn_Wv': _L0_attn_in['Wv'], 'L0_attn_Wa': _L0_attn_in['Wa'], 'L0_attn_Wb': _L0_attn_in['Wb'], 'L0_attn_Wg': _L0_attn_in['Wg'], 'L0_attn_dt_bias': _L0_attn_in['dt_bias'], 'L0_attn_A_log': _L0_attn_in['A_log'], 'L0_attn_conv_q_w': _L0_attn_in['conv_q_w'], 'L0_attn_conv_k_w': _L0_attn_in['conv_k_w'], 'L0_attn_conv_v_w': _L0_attn_in['conv_v_w'], 'L0_attn_gnorm_w': _L0_attn_in['gnorm_w'], 'L0_attn_Wo': _L0_attn_in['Wo'], 'L0_attn_W1': _L0_attn_in['W1'], 'L0_attn_W3': _L0_attn_in['W3'], 'L0_attn_W2': _L0_attn_in['W2'], 'L0_ffn_gate_w': _L0_ffn_in['gate_w'], 'L0_ffn_w1': _L0_ffn_in['w1'], 'L0_ffn_b1': _L0_ffn_in['b1'], 'L0_ffn_w2': _L0_ffn_in['w2'], 'L0_ffn_b2': _L0_ffn_in['b2'], 'L0_ffn_shared_w1': _L0_ffn_in['shared_w1'], 'L0_ffn_shared_b1': _L0_ffn_in['shared_b1'], 'L0_ffn_shared_w2': _L0_ffn_in['shared_w2'], 'L0_ffn_shared_b2': _L0_ffn_in['shared_b2'], 'L0_c': _L0_c, 'L0_wmod': _L0_wmod}
    _x0 = _d['L0_attn_x']
    _d['L0_attn_x'] = jax.random.normal(jax.random.fold_in(jax.random.key(seed), 1), (8, 256, 256), dtype=_x0.dtype)
    del _x0
    return _d

def reference(L0_attn_x, L0_attn_rms1_w, L0_attn_rms2_w, L0_attn_Wq, L0_attn_Wk, L0_attn_Wv, L0_attn_Wa, L0_attn_Wb, L0_attn_Wg, L0_attn_dt_bias, L0_attn_A_log, L0_attn_conv_q_w, L0_attn_conv_k_w, L0_attn_conv_v_w, L0_attn_gnorm_w, L0_attn_Wo, L0_attn_W1, L0_attn_W3, L0_attn_W2, L0_ffn_gate_w, L0_ffn_w1, L0_ffn_b1, L0_ffn_w2, L0_ffn_b2, L0_ffn_shared_w1, L0_ffn_shared_b1, L0_ffn_shared_w2, L0_ffn_shared_b2, L0_c, L0_wmod):

    def _L0_attn_ref(x, rms1_w, rms2_w, Wq, Wk, Wv, Wa, Wb, Wg, dt_bias, A_log, conv_q_w, conv_k_w, conv_v_w, gnorm_w, Wo, W1, W3, W2):
        import jax, jax.numpy as jnp
        import numpy as np
        B, T, D = (2, 128, 256)
        H, DK, DV = (32, 48, 96)
        KD, VD = (H * DK, H * DV)
        CS = 4
        INTER = 704
        EPS = 1e-05

        def rmsnorm(x, w, eps=EPS):
            return x * jax.lax.rsqrt(jnp.mean(x * x, axis=-1, keepdims=True) + eps) * w

        def short_conv(x, w):
            K = w.shape[1]
            xp = jnp.pad(x, ((0, 0), (K - 1, 0), (0, 0)))
            out = sum((xp[:, k:k + x.shape[1], :] * w[:, k] for k in range(K)))
            return jax.nn.silu(out)

        def l2norm(x, eps=1e-06):
            return x * jax.lax.rsqrt(jnp.sum(x * x, axis=-1, keepdims=True) + eps)

        def gated_delta_rule(q, k, v, g, beta):
            scale = q.shape[-1] ** (-0.5)

            def step(S, inp):
                qt, kt, vt, gt, bt = inp
                S = S * jnp.exp(gt)[..., None, None]
                mem = jnp.einsum('bhk,bhkv->bhv', kt, S)
                delta = (vt - mem) * bt[..., None]
                S = S + jnp.einsum('bhk,bhv->bhkv', kt, delta)
                o = jnp.einsum('bhk,bhkv->bhv', qt * scale, S)
                return (S, o)
            S0 = jnp.zeros((q.shape[0], q.shape[2], q.shape[3], v.shape[3]), q.dtype)
            xs = (q.transpose(1, 0, 2, 3), k.transpose(1, 0, 2, 3), v.transpose(1, 0, 2, 3), g.transpose(1, 0, 2), beta.transpose(1, 0, 2))
            _, o = jax.lax.scan(step, S0, xs)
            return o.transpose(1, 0, 2, 3)
        b, t, _ = x.shape
        h = rmsnorm(x, rms1_w)
        q = short_conv(h @ Wq, conv_q_w).reshape(b, t, H, DK)
        k = short_conv(h @ Wk, conv_k_w).reshape(b, t, H, DK)
        v = short_conv(h @ Wv, conv_v_w).reshape(b, t, H, DV)
        q, k = (l2norm(q), l2norm(k))
        g = -jnp.exp(A_log) * jax.nn.softplus(h @ Wa + dt_bias)
        beta = jax.nn.sigmoid(h @ Wb)
        o = gated_delta_rule(q, k, v, g, beta)
        gate = (h @ Wg).reshape(b, t, H, DV)
        o = rmsnorm(o, gnorm_w) * jax.nn.silu(gate)
        o = o.reshape(b, t, VD) @ Wo
        h2 = x + o
        ff = rmsnorm(h2, rms2_w)
        out = h2 + jax.nn.silu(ff @ W1) * (ff @ W3) @ W2
        return out

    def _L0_ffn_ref(x, gate_w, w1, b1, w2, b2, shared_w1, shared_b1, shared_w2, shared_b2):
        import jax, jax.numpy as jnp
        import numpy as np
        K = 2

        def gelu(v):
            return jax.nn.gelu(v, approximate=False)
        B, S, D = x.shape
        E = gate_w.shape[1]
        xf = x.reshape(-1, D)
        logits = xf @ gate_w
        top_logits, top_idx = jax.lax.top_k(logits, K)
        top_gates = jax.nn.softmax(top_logits, axis=-1)
        gates = jnp.sum(jax.nn.one_hot(top_idx, E, dtype=xf.dtype) * top_gates[..., None], axis=1)
        h = gelu(jnp.einsum('nd,edh->neh', xf, w1) + b1)
        out_e = jnp.einsum('neh,ehd->ned', h, w2) + b2
        routed = jnp.einsum('ne,ned->nd', gates, out_e)
        shared = gelu(xf @ shared_w1 + shared_b1) @ shared_w2 + shared_b2
        return (routed + shared).reshape(B, S, D)
    x = L0_attn_x
    mod = (_silu(L0_c) @ L0_wmod).reshape(L0_c.shape[0], 6, 1, -1)
    sa, ca, ga, sb, cb, gb = (mod[:, 0], mod[:, 1], mod[:, 2], mod[:, 3], mod[:, 4], mod[:, 5])
    ga = (2 * (ga >= 0) - 1) * jnp.maximum(jnp.abs(ga), 0.25)
    gb = (2 * (gb >= 0) - 1) * jnp.maximum(jnp.abs(gb), 0.25)
    h = _layernorm(x, axis=-1) * (1 + ca) + sa
    x = x + ga * _L0_attn_ref(h, L0_attn_rms1_w, L0_attn_rms2_w, L0_attn_Wq, L0_attn_Wk, L0_attn_Wv, L0_attn_Wa, L0_attn_Wb, L0_attn_Wg, L0_attn_dt_bias, L0_attn_A_log, L0_attn_conv_q_w, L0_attn_conv_k_w, L0_attn_conv_v_w, L0_attn_gnorm_w, L0_attn_Wo, L0_attn_W1, L0_attn_W3, L0_attn_W2)
    h = _layernorm(x, axis=-1) * (1 + cb) + sb
    x = x + gb * _L0_ffn_ref(h, L0_ffn_gate_w, L0_ffn_w1, L0_ffn_b1, L0_ffn_w2, L0_ffn_b2, L0_ffn_shared_w1, L0_ffn_shared_b1, L0_ffn_shared_w2, L0_ffn_shared_b2)
    return x

_drawn_inputs = setup_inputs


def setup_inputs(seed=0):
    import zlib

    import numpy as np

    out = dict(_drawn_inputs(seed))
    spreads = {'L0_attn_rms1_w': (1.0, 0.6), 'L0_attn_rms2_w': (1.0, 0.6), 'L0_attn_gnorm_w': (1.0, 0.6)}
    factors = {'L0_attn_Wa': 8.0,
     'L0_attn_Wb': 8.0,
     'L0_attn_dt_bias': 4.233,
     'L0_attn_A_log': 5.376,
     'L0_attn_W1': 7.549,
     'L0_attn_W3': 7.484,
     'L0_attn_W2': 7.481,
     'L0_ffn_gate_w': 60.048,
     'L0_ffn_w1': 64.0,
     'L0_ffn_b1': 64.0,
     'L0_ffn_w2': 64.0,
     'L0_ffn_b2': 49.824,
     'L0_ffn_shared_w1': 64.0,
     'L0_ffn_shared_b1': 64.0,
     'L0_ffn_shared_w2': 64.0,
     'L0_ffn_shared_b2': 49.752}
    for name, (base, spread) in spreads.items():
        noise = np.random.default_rng([zlib.crc32(name.encode()), seed]).standard_normal(out[name].shape)
        drawn = base * np.exp(spread * noise) if base else spread * noise
        out[name] = jnp.asarray(drawn.astype(out[name].dtype))
    for name, factor in factors.items():
        out[name] = (out[name] * factor).astype(out[name].dtype)
    return out
```

```python
from contextlib import ExitStack

import concourse.bass as bass
from concourse import mybir

F32 = mybir.dt.float32
BF16 = mybir.dt.bfloat16
U32 = mybir.dt.uint32
ALU = mybir.AluOpType
ACT = mybir.ActivationFunctionType
AX_X = mybir.AxisListType.X

B, T, D = 8, 256, 256
H, DK, DV = 32, 48, 96
TAPS = 4
INTER = 704
E, HID = 8, 128
SH = 2 * HID
P = 128
KT = D // P
CH = T // P
QH = 4
NQ = H // QH
PAIRS = QH // 2
QV = QH * DV
VT = QV // P
STEPS = NQ * B
U = CH * QH
LEVELS = 7
REFINE = 2
NB = 3
TILES = B * T // P
GT = 4
GROUPS = TILES // GT
GTOK = GT * P
MT = (INTER + P - 1) // P
RMS_EPS = 1e-5
L2_EPS = 1e-6
ATANH = [1.0 / (2 * k + 1) for k in range(9)]

C_ID, C_MASK, C_HEAD, C_IOTA = 0, P, P * (1 + LEVELS), P * (1 + LEVELS) + 2
C_COLS = C_IOTA + E


def wait(eng, sem, value):
    if not (isinstance(value, int) and value <= 0):
        eng.wait_ge(sem, value)


def wait_apart(eng, sem, value, passed):
    if isinstance(value, int):
        wait(eng, sem, value)
    else:
        eng.wait_ge(sem, value)
        eng.sem_inc(passed, 1)


def groups(eng, turn):
    turn(0)
    with eng.Fori(1, GROUPS) as g:
        turn(g)


class Chain:

    def __init__(self, eng, sem, turn=0, per=0):
        self.eng, self.sem, self.base, self.per, self.n = eng, sem, turn * per, per, 0

    def link(self, ins):
        self.n += 1
        ins.then_inc(self.sem, 1)
        self.eng.wait_ge(self.sem, self.base + self.n)

    def add(self, ins):
        self.n += 1
        ins.then_inc(self.sem, 1)

    def sync(self):
        self.eng.wait_ge(self.sem, self.base + self.n)

    def sync_apart(self, passed):
        wait_apart(self.eng, self.sem, self.base + self.n, passed)

    def close(self):
        assert self.n == self.per, (self.n, self.per)


def bc(ap, axis, n):
    v = ap.unsqueeze(axis)
    shape = list(v.shape)
    shape[axis] = n
    return v.broadcast_to(shape)


def prepare(nc, A, mem, scr):
    with ExitStack() as ctx:
        sb = lambda name, shape, dt=F32: ctx.enter_context(nc.sbuf_tensor("p1_" + name, shape, dt))
        sem = lambda name: ctx.enter_context(nc.semaphore("p1_" + name))
        ps = ctx.enter_context(nc.psum_tensor("p1_ps", [P, 8, 512], F32))
        x1 = sb("x1", [P, TILES, D])
        modb = sb("modb", [P, B, 2 * D])
        ct = sb("ct", [P, KT, B])
        cs = sb("cs", [P, KT, B])
        wmod = sb("wmod", [P, KT, 6 * D])
        mod = sb("mod", [B, 6 * D])
        sgn = sb("sgn", [B, 6 * D])
        wab = sb("wab", [P, KT, 2 * H])
        w1c = sb("w1c", [P, KT])
        dtb = sb("dtb", [P, 1])
        alog = sb("alog", [P, 1])
        ea = sb("ea", [P, 1])
        st = sb("st", [P, GT, 6])
        mv = sb("mv", [P, GT, 2])
        var = sb("var", [P, GT])
        rstd = sb("rstd", [P, GT])
        ss = sb("ss", [P, GT])
        ms = sb("ms", [P, GT])
        rr = sb("rr", [P, GT])
        nh = sb("nh", [P, GT])
        sq = sb("sq", [P, GT, D])
        hn = sb("hn", [P, GT, D])
        tmp = {n: sb("t_" + n, [P, GTOK]) for n in ("z", "u", "m", "zz", "z2", "p", "q", "a", "b", "bc", "zero", "zb")}

        ld, ldx, mod_st, modb_ld, scr_st = (sem(n) for n in ("ld", "ldx", "mod_st", "modb_ld", "scr_st"))
        c_silu, mod_ps, mod_ok = (sem(n) for n in ("c_silu", "mod_ps", "mod_ok"))
        dve, half_ok = (sem(n) for n in ("dve", "half_ok"))
        var_ok, rstd_ok, h0_ok, ss_ok, ms_ok, rr_ok, hn_ok, tr_ps, ht_ok = (
            sem(n) for n in ("var_ok", "rstd_ok", "h0_ok", "ss_ok", "ms_ok", "rr_ok", "hn_ok", "tr_ps", "ht_ok"))
        z_ps, absz_ok, u_ok, sp_ok, a_ok, eb_ok, beta_ok, bt_ps, bcum_ok = (
            sem(n) for n in ("z_ps", "absz_ok", "u_ok", "sp_ok", "a_ok", "eb_ok", "beta_ok", "bt_ps", "bcum_ok"))
        acts, done, late, passed, passed_pool = (sem(n) for n in ("acts", "done", "late", "passed", "passed_pool"))
        NLD = 1 + 1 + 2 + 1 + 2 * GROUPS + 1

        block = ctx.enter_context(nc.Block())

        @block.sync
        def _(sp):
            sp.dma_start(mem["const"][:], A["consts"]).then_inc(ld, 16)
            sp.dma_start(ct[:], A["c"]).then_inc(ld, 16)
            sp.dma_start(wmod[:], A["wmod"].rearrange("(k p) n -> p k n", k=KT)).then_inc(ld, 16)
            sp.dma_start(wab[:, :, 0:H], A["Wa"].rearrange("(k p) n -> p k n", k=KT)).then_inc(ld, 16)
            sp.dma_start(wab[:, :, H:2 * H], A["Wb"].rearrange("(k p) n -> p k n", k=KT)).then_inc(ld, 16)
            sp.dma_start(w1c[:], A["rms1_w"]).then_inc(ld, 16)
            for g in range(GROUPS):
                sp.dma_start(dtb[H * g:H * (g + 1), :], A["dt_bias"].rearrange("(h a) -> h a", a=1)).then_inc(ld, 16)
                sp.dma_start(alog[H * g:H * (g + 1), :], A["A_log"].rearrange("(h a) -> h a", a=1)).then_inc(ld, 16)
            for g in range(GROUPS):
                sp.dma_start(x1[:, g * GT:(g + 1) * GT, :],
                             A["x"].rearrange("b (c p) d -> p (b c) d", p=P)[:, g * GT:(g + 1) * GT, :]).then_inc(ldx, 16)
            sp.wait_ge(mod_ok, 2)
            sp.dma_start(scr["mod"], mod[:]).then_inc(mod_st, 16)
            sp.wait_ge(mod_st, 16)
            sp.dma_start(modb[:], scr["mod"][:, 0:2 * D].partition_broadcast(P)).then_inc(modb_ld, 16)
            sp.wait_ge(a_ok, 1)
            for g in range(GROUPS):
                sp.dma_start(scr["a"][2 * g:2 * g + 2].rearrange("b h t -> h b t"),
                             tmp["a"][H * g:H * (g + 1), :].rearrange("h (b t) -> h b t", b=2)).then_inc(scr_st, 16)
            sp.wait_ge(bcum_ok, CH * 2)
            for g in range(GROUPS):
                sp.dma_start(scr["b"][2 * g:2 * g + 2].rearrange("b h t -> h b t"),
                             tmp["bc"][H * g:H * (g + 1), :].rearrange("h (b c t) -> h b c t", b=2, c=CH)[:, :, 1, :]
                             ).then_inc(scr_st, 16)
            sp.wait_ge(scr_st, 2 * GROUPS * 16)

        @block.tensor
        def _(pe):
            pe.wait_ge(ld, 16 * NLD + 0)
            pe.wait_ge(c_silu, 1)
            for n in range(3):
                for k in range(KT):
                    last = pe.matmul(ps[0:B, n, :], cs[:, k, :], wmod[:, k, n * 512:(n + 1) * 512],
                                     start=(k == 0), stop=(k == KT - 1))
            last.then_inc(mod_ps, 1)
            def turn(g):
                pe.wait_ge(hn_ok, (g + 1) * GT)
                wait(pe, ht_ok, g * KT)
                for k in range(KT):
                    for j in range(GT):
                        last = pe.transpose(ps[:, 3 + k, j * P:(j + 1) * P], hn[:, j, k * P:(k + 1) * P],
                                            mem["const"][:, C_ID:C_ID + P])
                    last.then_inc(tr_ps, 1)

            groups(pe, turn)
            pe.wait_ge(ht_ok, GROUPS * KT)
            pe.wait_ge(mod_ok, 2)
            for w in range(2):
                for g in range(GROUPS):
                    for k in range(KT):
                        last = pe.matmul(ps[H * g:H * (g + 1), w, :], wab[:, k, H * w:H * (w + 1)],
                                         mem["hT"][:, k, g * GTOK:(g + 1) * GTOK], start=(k == 0), stop=(k == KT - 1))
                last.then_inc(z_ps, 1)
            pe.wait_ge(beta_ok, 1)
            for j in range(GT):
                last = pe.transpose(ps[:, 2, j * P:(j + 1) * P], tmp["b"][:, j * P:(j + 1) * P],
                                    mem["const"][:, C_ID:C_ID + P])
            last.then_inc(bt_ps, 1)

        @block.gpsimd
        def _(pool):
            pool.memset(nh[:], -0.5).then_inc(half_ok, 1)
            pool.wait_ge(half_ok, 1)
            def turn(g):
                wait_apart(pool, var_ok, g + 1, passed_pool)
                pool.tensor_tensor(rstd[:], var[:], nh[:], ALU.pow).then_inc(rstd_ok, 1)
                wait_apart(pool, ms_ok, g + 1, passed_pool)
                pool.tensor_tensor(rr[:], ms[:], nh[:], ALU.pow).then_inc(rr_ok, 1)

            groups(pool, turn)

        @block.scalar
        def _(act):
            act.wait_ge(ld, 16 * NLD)
            act.activation(cs[:], ct[:], ACT.Silu).then_inc(c_silu, 1)
            def turn(g):
                act.wait_ge(h0_ok, (g + 1) * 2)
                for j in range(GT):
                    act.activation(sq[:, j, :], mem["acc"][:, g * GT + j, :], ACT.Square,
                                   accum_out=ss[:, j:j + 1]).then_inc(ss_ok, 1)
                for k in range(KT):
                    act.wait_ge(tr_ps, g * KT + k + 1)
                    act.activation(mem["hT"][:, k, bass.ts(g, GTOK)], ps[:, 3 + k, :], ACT.Copy,
                                   scale=w1c[:, k:k + 1]).then_inc(ht_ok, 1)

            groups(act, turn)
            act.activation(ea[:], alog[:], ACT.Exp).then_inc(acts, 1)
            act.wait_ge(absz_ok, 1)
            act.activation(tmp["u"][:], tmp["p"][:], ACT.Exp, scale=-1.0).then_inc(u_ok, 1)
            act.wait_ge(z_ps, 2)
            act.activation(tmp["zb"][:], ps[:, 1, :], ACT.Exp, scale=-1.0).then_inc(eb_ok, 1)
            act.wait_ge(sp_ok, 1)
            act.activation(tmp["a"][:], tmp["z"][:], ACT.Exp, scale=-1.0).then_inc(a_ok, 1)

        @block.vector
        def _(v):
            c = Chain(v, dve)
            v.wait_ge(ld, 16 * NLD)
            const = mem["const"]
            v.memset(tmp["zero"][:], 0.0)
            v.tensor_copy(mem["id16"][:], const[:, C_ID:C_ID + P])
            v.tensor_copy(mem["mask"][:], const[:, C_MASK:C_MASK + LEVELS * P].rearrange("p (l n) -> p l n", l=LEVELS))
            v.wait_ge(mod_ps, 1)
            c.link(v.tensor_copy(mod[:], ps[0:B, 0:3, :].rearrange("b n m -> b (n m)")))
            for n in (1, 4):
                c.add(v.tensor_scalar(mod[:, n * D:(n + 1) * D], mod[:, n * D:(n + 1) * D], 1.0, None, ALU.add))
            for n in (2, 5):
                c.add(v.tensor_scalar(sgn[:, n * D:(n + 1) * D], mod[:, n * D:(n + 1) * D], 0.0, 2.0, ALU.is_ge, ALU.mult))
            c.sync()
            for n in (2, 5):
                ns = slice(n * D, (n + 1) * D)
                c.link(v.tensor_scalar(sgn[:, ns], sgn[:, ns], -1.0, None, ALU.add))
                c.link(v.tensor_tensor(mod[:, ns], mod[:, ns], sgn[:, ns], ALU.mult))
                v.scalar_tensor_tensor(mod[:, ns], mod[:, ns], 0.25, sgn[:, ns], ALU.max, ALU.mult).then_inc(mod_ok, 1)
            v.wait_ge(modb_ld, 16)
            v.wait_ge(ldx, 16 * GROUPS)
            def turn(g):
                c = Chain(v, done, g, 3 * GT + 2)
                acc = mem["acc"]
                for j in range(GT):
                    c.add(v.bn_stats(st[:, j, :], x1[:, g * GT + j, :]))
                c.sync_apart(passed)
                for j in range(GT):
                    c.add(v.bn_aggr(mv[:, j, :], st[:, j, :]))
                c.sync()
                v.tensor_scalar(var[:], mv[:, :, 1], RMS_EPS, None, ALU.add).then_inc(var_ok, 1)
                v.wait_ge(rstd_ok, g + 1)
                for j in range(GT):
                    c.add(v.tensor_scalar(acc[:, g * GT + j, :], x1[:, g * GT + j, :], mv[:, j, 0:1], rstd[:, j:j + 1],
                                          ALU.subtract, ALU.mult))
                c.sync()
                for half, op in ((1, ALU.mult), (0, ALU.add)):
                    for b2 in range(2):
                        v2 = acc[:, bass.ds(g * GT + 2 * b2, 2), :]
                        ins = v.tensor_tensor(v2, v2, bc(modb[:, g * 2 + b2, half * D:(half + 1) * D], 1, 2), op)
                        if half:
                            c.add(ins)
                        else:
                            ins.then_inc(h0_ok, 1)
                    c.sync()
                v.wait_ge(ss_ok, (g + 1) * GT)
                v.tensor_scalar(ms[:], ss[:], 1.0 / D, RMS_EPS, ALU.mult, ALU.add).then_inc(ms_ok, 1)
                v.wait_ge(rr_ok, g + 1)
                wait(v, tr_ps, g * KT)
                for j in range(GT):
                    v.tensor_scalar(hn[:, j, :], acc[:, g * GT + j, :], rr[:, j:j + 1], None, ALU.mult).then_inc(hn_ok, 1)
                c.close()

            groups(v, turn)
            t = tmp
            c = Chain(v, late)
            v.wait_ge(z_ps, 1)
            c.link(v.tensor_scalar(t["z"][:], ps[:, 0, :], dtb[:, 0:1], None, ALU.add))
            v.scalar_tensor_tensor(t["p"][:], t["z"][:], -1.0, t["z"][:], ALU.mult, ALU.max).then_inc(absz_ok, 1)
            c.add(v.tensor_scalar(t["m"][:], t["z"][:], 0.0, None, ALU.max))
            v.wait_ge(u_ok, 1)
            c.link(v.tensor_scalar(t["p"][:], t["u"][:], 2.0, None, ALU.add))
            c.link(v.reciprocal(t["q"][:], t["p"][:]))
            c.link(v.tensor_tensor(t["zz"][:], t["u"][:], t["q"][:], ALU.mult))
            c.link(v.tensor_tensor(t["z2"][:], t["zz"][:], t["zz"][:], ALU.mult))
            c.link(v.tensor_scalar(t["p"][:], t["z2"][:], ATANH[-1], None, ALU.mult))
            for k in range(len(ATANH) - 2, 0, -1):
                c.link(v.scalar_tensor_tensor(t["p"][:], t["p"][:], ATANH[k], t["z2"][:], ALU.add, ALU.mult))
            c.link(v.scalar_tensor_tensor(t["p"][:], t["p"][:], 1.0, t["zz"][:], ALU.add, ALU.mult))
            c.link(v.scalar_tensor_tensor(t["p"][:], t["p"][:], 2.0, t["m"][:], ALU.mult, ALU.add))
            v.wait_ge(acts, 1)
            v.tensor_scalar(t["z"][:], t["p"][:], ea[:, 0:1], None, ALU.mult).then_inc(sp_ok, 1)
            v.wait_ge(eb_ok, 1)
            c.link(v.tensor_scalar(t["q"][:], t["zb"][:], 1.0, None, ALU.add))
            v.reciprocal(t["b"][:], t["q"][:]).then_inc(beta_ok, 1)
            v.wait_ge(a_ok, 1)
            for n in range(2 * CH):
                v.tensor_tensor_scan(t["bc"][:, n * P:(n + 1) * P], t["a"][:, n * P:(n + 1) * P],
                                     t["zero"][:, n * P:(n + 1) * P], 1.0, ALU.mult, ALU.add).then_inc(bcum_ok, 1)
            v.wait_ge(bt_ps, 1)
            for j in range(GT):
                out = mem["beta"][:].rearrange("p (q g a) (c h) -> p a c g q h", q=NQ, g=GROUPS, c=CH)[:, j // 2, j % 2]
                src = ps[:, 2, j * P:(j + 1) * P].rearrange("p (g q h) -> p g q h", g=GROUPS, q=NQ)
                c.add(v.tensor_copy(out, src))
            c.sync()


def delta_rule(nc, A, mem, scr):
    with ExitStack() as ctx:
        sb = lambda name, shape, dt=F32: ctx.enter_context(nc.sbuf_tensor("dr_" + name, shape, dt))
        sem = lambda name: ctx.enter_context(nc.semaphore("dr_" + name))
        ps = ctx.enter_context(nc.psum_tensor("dr_ps", [P, 8, 512], F32))
        A0, A1, X0, X1, X2, CW, CX, CO = range(8)

        hb = sb("hb", [P, NB, KT, T])
        abc = sb("abc", [P, NB, QH, T])
        bcb = sb("bcb", [P, NB, PAIRS, P])
        wqk = sb("wqk", [P, KT, 2 * PAIRS, P])
        wv = sb("wv", [P, KT, QV])
        wg = sb("wg", [P, KT, QV])
        cw = sb("cw", [P, 2 * PAIRS + VT, TAPS])
        wo = sb("wo", [P, NQ * VT, D])
        gw = sb("gw", [P, VT])
        y = sb("y", [P, 4, T])
        qk = sb("qk", [P, PAIRS, CH, 2, P])
        vT = sb("vT", [P, VT, T])
        sq = sb("sq", [P, 2, PAIRS, T])
        dec = sb("dec", [P, U, P])
        am = sb("am", [P, NB, U, 2, P])
        b16 = sb("b16", [P, NB, U, P], BF16)
        tn = sb("tn", [P, U, P], BF16)
        tt = sb("tt", [P, U, P], BF16)
        w16 = sb("w16", [P, U, P], BF16)
        tf = sb("tf", [P, NB, U, P], BF16)
        rhs = sb("rhs", [P, NB, CH, QV])
        rhs16 = sb("rhs16", [P, NB, CH, QV], BF16)
        kg = sb("kg", [P, NB, QH, 64])
        kqb = sb("kqb", [P, NB, PAIRS, 2, P])
        gs = sb("gs", [P, NB, CH, QV])
        w = sb("w", [P, CH, QV])
        r16 = sb("r16", [P, QV], BF16)
        S = sb("S", [P, PAIRS, 2 * DV])
        og = sb("og", [P, CH, QV])
        oT = sb("oT", [P, VT, P])
        sqo = sb("sqo", [P, QV])
        kk = sb("kk", [P, U])
        rkk = sb("rkk", [P, U])
        gam = sb("gam", [P, NB, U])
        nrm = sb("nrm", [P, NB, U])
        e2 = sb("e2", [P, NB, U])
        cj = sb("cj", [P, QH])
        mso = sb("mso", [P, QH])
        vo = sb("vo", [P, QH])
        fo = sb("fo", [P, QH])
        half = sb("half", [P, U])
        nhalf = sb("nhalf", [P, QH])

        names = """w_ld h_ld a_ld b_ld c_ld set_ok qk_ps v_ps g_ps n_ps kt_ps kk_ps vt_ps
            tap0 tap qk_ok v_ok sq_ok nk rk gam_ok e2_ok nrm_ok cj_ok kg_ok gs_ok dec_ok am_ok b16_c b16_ok ia_ok
            kqb_ok r_ok r16_ok p1 p2 p3 mask_ok tn_ok tt_ok
            w0_ps res_ps d_ps s_ps ks_ps o_ps ot_ps wo_ps w_ok rs_ok S_ok r1_ok r1h_ok sqo_ok mso_ok vo_ok fo_ok
            og_ok oT_ok acc_ok passed_pool passed_sp""".split()
        s = {n: sem(n) for n in names}
        WDMAS = KT * 2 + 2 + 2 * QH + 1
        const, id16, mask = mem["const"], mem["id16"], mem["mask"]
        ident = const[:, C_ID:C_ID + P]
        NT = 2 * PAIRS + VT

        block = ctx.enter_context(nc.Block())

        def steps(eng, turn):
            turn((0, 0), None, None)
            turn((1, 1), (0, 0), None)
            full = STEPS - 2
            loops = full // NB
            with eng.Fori(0, loops) as i:
                for m in range(NB):
                    turn((i * NB + m + 2, (m + 2) % NB), (i * NB + m + 1, (m + 1) % NB), (i * NB + m, m))
            for t in range(loops * NB, full):
                turn((t + 2, (t + 2) % NB), (t + 1, (t + 1) % NB), (t, t % NB))
            t = STEPS - 1
            turn(None, (t, t % NB), (t - 1, (t - 1) % NB))
            turn(None, None, (t, t % NB))

        def slots(a, b, c, on):
            first_c = [("w0", 0), ("delta", 0, 0), ("delta", 0, 1), ("ks",), ("residual", 1, 0), ("residual", 1, 1), ("out", 1)]
            second_c = [("residual", 0, 0), ("residual", 0, 1), ("state_out",), ("w0", 1), ("delta", 1, 0), ("delta", 1, 1),
                        ("finish", 1)]
            first_a = [("qk", 0), ("v", 0), ("v", 1), ("gate", 0), ("gate", 1), ("scores", 1), ("values", 0)]
            second_a = [("qk", 1), None, ("norms",), ("keys",), ("scores", 0), None, ("values", 1)]
            middle_c = {4: ("oT", 0), 5: ("wo", 0)}
            for l in range(LEVELS):
                if b:
                    on["merge1"](b, l, 0)
                    on["merge1"](b, l, 1)
                if c and first_c[l]:
                    on[first_c[l][0]](c, *first_c[l][1:])
                if a and first_a[l]:
                    on[first_a[l][0]](a, *first_a[l][1:])
                if b:
                    on["merge2"](b, l, 0)
                if c and l in middle_c:
                    on[middle_c[l][0]](c, *middle_c[l][1:])
                if c and second_c[l]:
                    on[second_c[l][0]](c, *second_c[l][1:])
                if a and second_a[l]:
                    on[second_a[l][0]](a, *second_a[l][1:])
                if b:
                    on["merge2"](b, l, 1)

        def run(eng, on):
            steps(eng, lambda a, b, c: slots(a, b, c, on))

        def nothing(*_):
            return None

        PIECES = ("merge1", "merge2", "w0", "delta", "residual", "ks", "out", "state_out", "oT", "wo", "finish",
                  "qk", "v", "gate", "scores", "values", "norms", "keys")

        @block.sync
        def _(sp):
            sp.dma_start(wo[:], A["Wo"].rearrange("(t p) n -> p t n", p=P)).then_inc(s["c_ld"], 16)
            sp.dma_start(gw[:], A["gnorm_w"]).then_inc(s["c_ld"], 16)

            sp.wait_ge(s["set_ok"], 6)

            def weights(q):
                wait_apart(sp, s["v_ps"], q * B * 2, s["passed_sp"])
                wait_apart(sp, s["g_ps"], q * B * 2, s["passed_sp"])
                wait_apart(sp, s["v_ok"], q * B * VT, s["passed_sp"])
                for k in range(KT):
                    for n, name in enumerate(("Wq", "Wk")):
                        sp.dma_start(wqk[:, k, 2 * n:2 * n + 2, :].rearrange("p a (h d) -> p (a h) d", h=2)[:, :, 0:DK],
                                     A[name][k * P:(k + 1) * P, bass.ds(q * (QH * DK), QH * DK)]
                                     .rearrange("p (h d) -> p h d", d=DK)).then_inc(s["w_ld"], 16)
                for wt, name in ((wv, "Wv"), (wg, "Wg")):
                    sp.dma_start(wt[:], A[name][:, bass.ds(q * QV, QV)].rearrange("(k p) n -> p k n", k=KT)
                                 ).then_inc(s["w_ld"], 16)
                for n, name in enumerate(("conv_q_w", "conv_k_w")):
                    for h in range(QH):
                        sp.dma_start(cw[64 * (h % 2):64 * (h % 2) + DK, 2 * n + h // 2, :],
                                     A[name][bass.ds(q * (QH * DK) + h * DK, DK), :]).then_inc(s["w_ld"], 16)
                sp.dma_start(cw[:, 2 * PAIRS:, :], A["conv_v_w"][bass.ds(q * QV, QV), :].rearrange("(t p) k -> p t k", p=P)
                             ).then_inc(s["w_ld"], 16)

            def batch(q, b):
                it = q * B + b
                m = it % NB
                if not isinstance(it, int) or it >= NB:
                    wait_apart(sp, s["g_ps"], (it - NB + 1) * 2, s["passed_sp"])
                    wait_apart(sp, s["dec_ok"], (it - NB + 1) * U, s["passed_sp"])
                    wait_apart(sp, s["kqb_ok"], (it - NB + 1) * PAIRS, s["passed_sp"])
                wait_apart(sp, s["h_ld"], it * 16, s["passed_sp"])
                wait_apart(sp, s["a_ld"], it * 16, s["passed_sp"])
                wait_apart(sp, s["b_ld"], it * 32, s["passed_sp"])
                sp.dma_start(hb[:, m], mem["hT"][:, :, bass.ts(b, T)]).then_inc(s["h_ld"], 16)
                sp.dma_start(abc[:, m], scr["a"][b, bass.ds(q * QH, QH), :].partition_broadcast(P)).then_inc(s["a_ld"], 16)
                for side in range(2):
                    src = scr["b"][b, bass.ds(q * QH, QH), :].rearrange("(a s) t -> s a t", s=2)[side]
                    sp.dma_start(bcb[64 * side:64 * side + 64, m], src.partition_broadcast(64)).then_inc(s["b_ld"], 16)

            weights(0)
            for b in range(B):
                batch(0, b)
            with sp.Fori(1, NQ) as q:
                weights(q)
                with sp.Fori(0, B) as b:
                    batch(q, b)
            sp.wait_ge(s["acc_ok"], STEPS * CH + 1)

        @block.tensor
        def _(pe):
            on = {n: nothing for n in PIECES}

            def merge1(st, l, g):
                it, m = st
                if l == 0:
                    pe.wait_ge(s["b16_ok"], it * CH + g + 1)
                    if g == 0:
                        wait(pe, s["tt_ok"], (it * LEVELS - 1) * 2 + 1 if not isinstance(it, int) or it else 0)
                else:
                    pe.wait_ge(s["tt_ok"], (it * LEVELS + l - 1) * 2 + g + 1)
                    if l > 1:
                        pe.wait_ge(s["tn_ok"], (it * (LEVELS - 2) + l - 2) * 2 + g + 1)
                for u in range(QH * g, QH * g + QH):
                    last = pe.matmul(ps[:, (X0, X1)[g], (u % QH) * P:(u % QH + 1) * P], b16[:, m, u, :],
                                     id16[:] if l == 0 else tn[:, u, :], start=True, stop=True)
                last.then_inc(s["p1"], 1)

            def merge2(st, l, g):
                it, m = st
                pe.wait_ge(s["mask_ok"], (it * LEVELS + l) * 2 + g + 1)
                if g == 0:
                    wait(pe, s["tt_ok"], (it * LEVELS + l) * 2 if not isinstance(it, int) or it or l else 0)
                middle = 0 < l < LEVELS - 1
                us = range(QH * g, QH * g + QH)
                if middle:
                    for u in us:
                        last = pe.matmul(ps[:, (X2, X1)[g], (u % QH) * P:(u % QH + 1) * P], tt[:, u, :], w16[:, u, :],
                                         start=True, stop=True)
                    last.then_inc(s["p2"], 1)
                    if g == 1:
                        pe.wait_ge(s["tn_ok"], (it * (LEVELS - 2) + l - 1) * 2 + 1)
                wt = tn if l == 0 else w16
                for u in us:
                    last = pe.matmul(ps[:, (X0, X2)[g], (u % QH) * P:(u % QH + 1) * P], wt[:, u, :],
                                     id16[:] if l == 0 else tt[:, u, :], start=True, stop=True)
                last.then_inc(s["p3"], 1)

            def project(bank, off, wt, m):
                for k in range(KT):
                    last = pe.matmul(ps[:, bank, off:off + T], wt(k), hb[:, m, k, :], start=(k == 0), stop=(k == KT - 1))
                return last

            def qk_(st, n):
                it, m = st
                if n == 0:
                    pe.wait_ge(s["w_ld"], (it // B + 1) * (16 * WDMAS))
                    pe.wait_ge(s["h_ld"], (it + 1) * 16)
                wait(pe, s["r_ok"], it * CH if n else it * CH - 1 if not isinstance(it, int) or it else 0)
                for a in range(PAIRS):
                    last = project((A0, A1)[n], a * T, lambda k: wqk[:, k, 2 * n + a, :], m)
                last.then_inc(s["qk_ps"], 1)

            def v_(st, n):
                it, m = st
                pe.wait_ge(s["qk_ok"], it * 2 * PAIRS + PAIRS * (n + 1))
                for j, t in enumerate((range(2), range(2, VT))[n]):
                    last = project((A0, A1)[n], j * T, lambda k: wv[:, k, t * P:(t + 1) * P], m)
                last.then_inc(s["v_ps"], 1)

            def norms(st):
                it, m = st
                pe.wait_ge(s["v_ok"], it * VT + 2)
                pe.wait_ge(s["sq_ok"], (it + 1) * 2 * PAIRS)
                for c in range(CH):
                    for n in range(2):
                        for a in range(PAIRS):
                            at = c * 2 * QH + n * QH + 2 * a
                            last = pe.matmul(ps[:, A0, at:at + 2], sq[:, n, a, c * P:(c + 1) * P],
                                             const[:, C_HEAD:C_HEAD + 2], start=True, stop=True)
                last.then_inc(s["n_ps"], 1)

            def gate(st, c):
                it, m = st
                if c == 0:
                    pe.wait_ge(s["v_ok"], (it + 1) * VT)
                else:
                    pe.wait_ge(s["rk"], it + 1)
                for k in range(KT):
                    last = pe.matmul(ps[:, (A1, A0)[c], 0:QV], hb[:, m, k, c * P:(c + 1) * P], wg[:, k, :],
                                     start=(k == 0), stop=(k == KT - 1))
                last.then_inc(s["g_ps"], 1)

            def keys(st):
                it, m = st
                pe.wait_ge(s["gs_ok"], it * CH + 1)
                for a in range(PAIRS):
                    last = pe.transpose(ps[:, A1, a * P:(a + 1) * P], qk[:, a, 0, 0, :], ident)
                last.then_inc(s["kt_ps"], 1)

            def scores(st, c):
                it, m = st
                for side in range(2):
                    if c == 0:
                        pe.wait_ge(*((s["gs_ok"], it * CH + 2), (s["kg_ok"], it + 1))[side])
                    else:
                        pe.wait_ge(s["am_ok"], it * 4 + side + 1)
                for a in range(PAIRS):
                    for side in range(2):
                        lo = 64 * side
                        last = pe.matmul(ps[:, (A0, A1)[side], a * 2 * P:(a + 1) * 2 * P], qk[lo:lo + 64, a, c, 0, :],
                                         qk[lo:lo + 64, a, c, :, :].rearrange("p n t -> p (n t)"), start=True, stop=True)
                last.then_inc(s["kk_ps"], 1)

            def values(st, c):
                it, m = st
                if c == 0:
                    pe.wait_ge(s["v_ok"], (it + 1) * VT)
                pe.wait_ge(s["am_ok"], it * 4 + 2 + c + 1)
                for t in range(VT):
                    last = pe.transpose(ps[:, (A0, A1)[c], t * P:(t + 1) * P], vT[:, t, c * P:(c + 1) * P], ident)
                last.then_inc(s["vt_ps"], 1)

            def heads(bank, wt, x, start):
                for h in range(QH):
                    last = pe.matmul(ps[:, bank, h * DV:(h + 1) * DV], wt(h), x[:, h * DV:(h + 1) * DV],
                                     start=(start and h == 0), stop=(h == QH - 1), skip_group_check=True)
                return last

            def w0(st, c):
                it, m = st
                pe.wait_ge(s["tt_ok"], ((it + 1) * LEVELS - 1) * 2 + c + 1)
                pe.wait_ge(s["r16_ok"], it + 1) if c == 0 else pe.wait_ge(s["r1h_ok"], it + 1)
                heads(CW, lambda h: tf[:, m, c * QH + h, :], rhs16[:, m, c, :], True).then_inc(s["w0_ps"], 1)

            def residual(st, c, r):
                it, m = st
                pe.wait_ge(s["w_ok"], (it * 2 + c) * (REFINE + 1) + r + 1)
                if c == 0 and r == 0:
                    pe.wait_ge(s["acc_ok"], it * CH + 1)
                elif c == 1 and r == 0:
                    pe.wait_ge(s["r1_ok"], it + 1)
                elif c == 1 and r == 1:
                    pe.wait_ge(s["oT_ok"], (it * CH + 1) * VT)
                pe.wait_ge(s["ia_ok"], it * CH + c + 1)
                heads(CX, lambda h: am[:, m, c * QH + h, 0, :], w[:, c, :], True).then_inc(s["res_ps"], 1)

            def delta(st, c, r):
                it, m = st
                pe.wait_ge(s["rs_ok"], (it * 2 + c) * REFINE + r + 1)
                heads(CW, lambda h: tf[:, m, c * QH + h, :], r16, False).then_inc(s["d_ps"], 1)

            def outputs(st, c):
                it, m = st
                pe.wait_ge(s["w_ok"], (it * 2 + c + 1) * (REFINE + 1))
                if c == 1:
                    pe.wait_ge(s["og_ok"], (it * CH + 1) * QH)
                    for a in range(PAIRS):
                        pe.matmul(ps[:, CO, a * 2 * DV:(a + 1) * 2 * DV], kqb[:, m, a, 1, :], S[:, a, :],
                                  start=(a == 0), stop=False, skip_group_check=True)
                heads(CO, lambda h: am[:, m, c * QH + h, 1, :], w[:, c, :], c == 0).then_inc(s["o_ps"], 1)

            def state_out(st):
                it, m = st
                pe.wait_ge(s["w_ok"], (it * 2 + 1) * (REFINE + 1))
                pe.wait_ge(s["rs_ok"], (it * 2 + 1) * REFINE)
                for h in range(QH):
                    lo, at = 64 * (h % 2), (h // 2) * 2 * DV + (h % 2) * DV
                    last = pe.matmul(ps[lo:lo + 64, CX, at:at + DV], kg[:, m, h, :], w[:, 0, h * DV:(h + 1) * DV],
                                     start=True, stop=True, skip_group_check=True)
                last.then_inc(s["s_ps"], 1)
                outputs(st, 0)

            def ks(st):
                it, m = st
                pe.wait_ge(s["S_ok"], (it + 1) * 2)
                for a in range(PAIRS):
                    last = pe.matmul(ps[:, CX, a * 2 * DV:(a + 1) * 2 * DV], kqb[:, m, a, 0, :], S[:, a, :],
                                     start=True, stop=True)
                last.then_inc(s["ks_ps"], 1)

            def turn_out(st, c):
                it, m = st
                pe.wait_ge(s["og_ok"], (it * CH + c + 1) * QH)
                if c == 0:
                    pe.wait_ge(s["rs_ok"], (it * 2 + 1) * REFINE + 1)
                else:
                    pe.wait_ge(s["acc_ok"], it * CH + 2)
                for t in range(VT):
                    last = pe.transpose(ps[:, CX, t * P:(t + 1) * P], og[:, c, t * P:(t + 1) * P], ident)
                last.then_inc(s["ot_ps"], 1)

            def wo_(st, c):
                it, m = st
                pe.wait_ge(s["oT_ok"], (it * CH + c + 1) * VT)
                if c == 0:
                    pe.wait_ge(s["rs_ok"], (it * 2 + 2) * REFINE)
                for t in range(VT):
                    last = pe.matmul(ps[:, CX, 0:D], oT[:, t, :], wo[:, (it // B) * VT + t, :],
                                     start=(t == 0), stop=(t == VT - 1))
                last.then_inc(s["wo_ps"], 1)

            def finish(st, c):
                turn_out(st, 1)
                wo_(st, 1)

            on.update(merge1=merge1, merge2=merge2, qk=qk_, v=v_, norms=norms, gate=gate, keys=keys, scores=scores,
                      values=values, w0=w0, residual=residual, delta=delta, out=outputs, state_out=state_out, ks=ks,
                      oT=turn_out, wo=wo_, finish=finish)
            pe.wait_ge(s["c_ld"], 32)
            run(pe, on)

        @block.vector
        def _(v):
            on = {n: nothing for n in PIECES}

            def merge1(st, l, g):
                it, m = st
                pe_done = (it * LEVELS + l) * 2 + g + 1
                v.wait_ge(s["p1"], pe_done)
                wait(v, s["p3"], pe_done - 2 if not isinstance(pe_done, int) or pe_done > 2 else 0)
                us = slice(QH * g, QH * g + QH)
                v.tensor_tensor((tn if l == 0 else w16)[:, us, :], ps[:, (X0, X1)[g], :].rearrange("p (u n) -> p u n", u=QH),
                                bc(mask[:, l, :], 1, QH), ALU.mult).then_inc(s["mask_ok"], 1)

            def taps(it, base, bank, tiles):
                n = len(tiles)
                for x in range(1, TAPS):
                    for j, (t, slot, off) in enumerate(tiles):
                        if x == 1:
                            v.wait_ge(s["tap0"], it * NT + base + n)
                        else:
                            v.wait_ge(s["tap"], it * NT * 3 + base * 3 + (x - 2) * n + j + 1)
                        v.scalar_tensor_tensor(y[:, slot, x:T], ps[:, bank, off:off + T - x],
                                               cw[:, t, TAPS - 1 - x:TAPS - x], y[:, slot, x:T],
                                               ALU.mult, ALU.add).then_inc(s["tap"], 1)

            def qk_(st, n):
                it, m = st
                v.wait_ge(s["qk_ps"], it * 2 + n + 1)
                taps(it, 2 * n, (A0, A1)[n], [(2 * n + a, 2 * n + a, a * T) for a in range(PAIRS)])
                if n == 0:
                    decays(st)

            def v_(st, n):
                it, m = st
                v.wait_ge(s["v_ps"], it * 2 + n + 1)
                taps(it, 4 + 2 * n, (A0, A1)[n],
                     [(4 + t, t, j * T) for j, t in enumerate((range(2), range(2, VT))[n])])

            def decays(st):
                it, m = st
                v.wait_ge(s["a_ld"], (it + 1) * 16)
                for u in range(U):
                    c, h = divmod(u, QH)
                    v.tensor_tensor_scan(dec[:, u, :], abc[:, m, h, c * P:(c + 1) * P], ident, 0.0,
                                         ALU.mult, ALU.add).then_inc(s["dec_ok"], 1)

            def norms(st):
                it, m = st
                v.wait_ge(s["n_ps"], it + 1)
                n4 = ps[:, A0, 0:2 * U].rearrange("p (c n h) -> p c n h", c=CH, n=2)
                v.tensor_scalar(kk[:].rearrange("p (c h) -> p c h", c=CH), n4[:, :, 0, :], L2_EPS, None,
                                ALU.add).then_inc(s["nk"], 1)
                v.tensor_scalar(e2[:, m].rearrange("p (c h) -> p c h", c=CH), n4[:, :, 1, :], L2_EPS, DK * RMS_EPS,
                                ALU.add, ALU.mult).then_inc(s["rk"], 1)
                v.wait_ge(s["nk"], it + 1)
                v.reciprocal(rkk[:], kk[:]).then_inc(s["e2_ok"], 1)
                v.wait_ge(s["e2_ok"], it + 1)
                v.tensor_tensor(gam[:, m], rkk[:], mem["beta"][:, it, :], ALU.mult).then_inc(s["gam_ok"], 1)

            def keys(st):
                it, m = st
                v.wait_ge(s["gam_ok"], it + 1)
                v.wait_ge(s["dec_ok"], (it + 1) * U)
                v.tensor_tensor(cj[:], gam[:, m, 0:QH], dec[:, 0:QH, P - 1], ALU.mult).then_inc(s["cj_ok"], 1)
                v.wait_ge(s["cj_ok"], it + 1)
                v.wait_ge(s["kt_ps"], it + 1)
                v.tensor_tensor(kg[:, m], ps[:, A1, 0:QH * 64].rearrange("p (h d) -> p h d", h=QH),
                                bc(cj[:], 2, 64), ALU.mult).then_inc(s["kg_ok"], 1)

            def scores(st, c):
                it, m = st
                v.wait_ge(s["kk_ps"], it * CH + c + 1)
                for side in range(2):
                    for a in range(PAIRS):
                        u = c * QH + 2 * a + side
                        ins = v.scalar_tensor_tensor(
                            am[:, m, u], ps[:, (A0, A1)[side], a * 2 * P:(a + 1) * 2 * P].rearrange("p (n t) -> p n t", n=2),
                            gam[:, m, u:u + 1], bc(dec[:, u, :], 1, 2), ALU.mult, ALU.mult)
                    ins.then_inc(s["am_ok"], 1)

            def values(st, c):
                it, m = st
                v.wait_ge(s["vt_ps"], it * CH + c + 1)
                v.wait_ge(s["nrm_ok"], it + 1)
                v.tensor_tensor(rhs[:, m, c].rearrange("p (h d) -> p h d", h=QH),
                                ps[:, (A0, A1)[c], 0:QV].rearrange("p (h d) -> p h d", h=QH),
                                bc(nrm[:, m, c * QH:(c + 1) * QH], 2, DV), ALU.mult).then_inc(s["r_ok"], 1)

            def residual(st, c, r):
                it, m = st
                v.wait_ge(s["res_ps"], (it * 2 + c) * REFINE + r + 1)
                v.tensor_tensor(r16[:], rhs[:, m, c], ps[:, CX, 0:QV], ALU.subtract).then_inc(s["rs_ok"], 1)

            def ks(st):
                it, m = st
                v.wait_ge(s["ks_ps"], it + 1)
                v.tensor_tensor(rhs[:, m, 1], rhs[:, m, 1], ps[:, CX, 0:QV], ALU.subtract).then_inc(s["r1_ok"], 1)

            def gated(st, c):
                it, m = st
                n = it * CH + c
                v.wait_ge(s["sqo_ok"], n + 1)
                v.tensor_reduce(mso[:], sqo[:].rearrange("p (h d) -> p h d", h=QH), AX_X, ALU.add).then_inc(s["mso_ok"], 1)
                v.wait_ge(s["mso_ok"], n + 1)
                v.scalar_tensor_tensor(vo[:], mso[:], 1.0 / DV, e2[:, m, c * QH:(c + 1) * QH], ALU.mult,
                                       ALU.add).then_inc(s["vo_ok"], 1)
                v.wait_ge(s["fo_ok"], n + 1)
                for h in range(QH):
                    hs = slice(h * DV, (h + 1) * DV)
                    v.scalar_tensor_tensor(og[:, c, hs], ps[:, CO, hs], fo[:, h:h + 1], gs[:, m, c, hs], ALU.mult,
                                           ALU.mult).then_inc(s["og_ok"], 1)

            def acc(st, c):
                it, m = st
                v.wait_ge(s["wo_ps"], it * CH + c + 1)
                at = mem["acc"][:, (it % B) * CH + c, :]
                v.tensor_tensor(at, at, ps[:, CX, 0:D], ALU.add).then_inc(s["acc_ok"], 1)

            on.update(merge1=merge1, qk=qk_, v=v_, norms=norms, keys=keys, scores=scores, values=values,
                      residual=residual, ks=ks, state_out=lambda st: gated(st, 0), out=gated,
                      wo=acc, finish=lambda st, c: acc(st, 1))
            v.memset(wqk[:], 0.0).then_inc(s["set_ok"], 1)
            v.memset(cw[:], 0.0).then_inc(s["set_ok"], 1)
            v.memset(S[:], 0.0).then_inc(s["set_ok"], 1)
            v.memset(mso[:], 0.0).then_inc(s["acc_ok"], 1)
            v.wait_ge(s["set_ok"], 6)
            run(v, on)

        @block.scalar
        def _(act):
            on = {n: nothing for n in PIECES}

            def merge2(st, l, g):
                it, m = st
                us = slice(QH * g, QH * g + QH)
                if 0 < l < LEVELS - 1:
                    act.wait_ge(s["p2"], (it * (LEVELS - 2) + l - 1) * 2 + g + 1)
                    act.copy(tn[:, us, :], ps[:, (X2, X1)[g], :].rearrange("p (u n) -> p u n", u=QH)).then_inc(s["tn_ok"], 1)
                act.wait_ge(s["p3"], (it * LEVELS + l) * 2 + g + 1)
                dst = tf[:, m, us, :] if l == LEVELS - 1 else tt[:, us, :]
                act.copy(dst, ps[:, (X0, X2)[g], :].rearrange("p (u n) -> p u n", u=QH)).then_inc(s["tt_ok"], 1)

            def conv(it, base, bank, tiles, store):
                for j, (t, slot, off) in enumerate(tiles):
                    act.activation(y[:, slot, :], ps[:, bank, off:off + T], ACT.Copy,
                                   scale=cw[:, t, TAPS - 1:TAPS]).then_inc(s["tap0"], 1)
                for j, (t, slot, off) in enumerate(tiles):
                    act.wait_ge(s["tap"], it * NT * 3 + base * 3 + 2 * len(tiles) + j + 1)
                    store(j, slot)

            def qk_(st, n):
                it, m = st
                act.wait_ge(s["qk_ps"], it * 2 + n + 1)
                wait(act, s["kk_ps"], it * CH)
                wait(act, s["kqb_ok"], it * PAIRS)

                def store(j, slot):
                    act.activation(qk[:, j, :, 1 - n, :], y[:, slot, :].rearrange("p (c t) -> p c t", c=CH),
                                   ACT.Silu).then_inc(s["qk_ok"], 1)
                conv(it, 2 * n, (A0, A1)[n], [(2 * n + a, 2 * n + a, a * T) for a in range(PAIRS)], store)
                wait(act, s["n_ps"], it)
                for a in range(PAIRS):
                    act.wait_ge(s["qk_ok"], it * 2 * PAIRS + n * PAIRS + a + 1)
                    act.activation(sq[:, 1 - n, a, :].rearrange("p (c t) -> p c t", c=CH), qk[:, a, :, 1 - n, :],
                                   ACT.Square).then_inc(s["sq_ok"], 1)

            def v_(st, n):
                it, m = st
                act.wait_ge(s["v_ps"], it * 2 + n + 1)
                wait(act, s["vt_ps"], it * CH)

                def store(j, slot):
                    act.activation(vT[:, slot, :], y[:, slot, :], ACT.Silu).then_inc(s["v_ok"], 1)
                conv(it, 4 + 2 * n, (A0, A1)[n],
                     [(4 + t, t, j * T) for j, t in enumerate((range(2), range(2, VT))[n])], store)

            def gate(st, c):
                it, m = st
                act.wait_ge(s["g_ps"], it * CH + c + 1)
                act.activation(gs[:, m, c, :], ps[:, (A1, A0)[c], 0:QV], ACT.Silu).then_inc(s["gs_ok"], 1)

            def scores(st, c):
                it, m = st
                act.wait_ge(s["am_ok"], it * 4 + 2 * c + 2)
                act.activation(b16[:, m, c * QH:(c + 1) * QH, :], am[:, m, c * QH:(c + 1) * QH, 0, :], ACT.Copy,
                               scale=-1.0).then_inc(s["b16_c"], 1)

            def values(st, c):
                it, m = st
                if c == 0:
                    act.wait_ge(s["r_ok"], it * CH + 1)
                    act.copy(rhs16[:, m, 0, :], rhs[:, m, 0, :]).then_inc(s["r16_ok"], 1)

            def copy_w(it, c, n):
                k = (it * 2 + c) * (REFINE + 1) + n + 1
                act.copy(w[:, c, :], ps[:, CW, 0:QV]).then_inc(s["w_ok"], 1)

            def w0(st, c):
                it, m = st
                act.wait_ge(s["w0_ps"], it * CH + c + 1)
                copy_w(it, c, 0)

            def delta(st, c, r):
                it, m = st
                act.wait_ge(s["d_ps"], (it * 2 + c) * REFINE + r + 1)
                copy_w(it, c, r + 1)

            def squares(st, c):
                it, m = st
                act.wait_ge(s["o_ps"], it * CH + c + 1)
                act.activation(sqo[:], ps[:, CO, 0:QV], ACT.Square).then_inc(s["sqo_ok"], 1)

            def state_out(st):
                it, m = st
                act.wait_ge(s["s_ps"], it + 1)
                for side in range(2):
                    lo = 64 * side
                    act.copy(S[lo:lo + 64, :, side * DV:(side + 1) * DV],
                             ps[lo:lo + 64, CX, 0:QV].rearrange("p (a n) -> p a n", a=PAIRS)[:, :, side * DV:(side + 1) * DV]
                             ).then_inc(s["S_ok"], 1)
                squares(st, 0)

            def ks(st):
                it, m = st
                act.wait_ge(s["r1_ok"], it + 1)
                act.copy(rhs16[:, m, 1, :], rhs[:, m, 1, :]).then_inc(s["r1h_ok"], 1)

            def turn_out(st, c):
                it, m = st
                act.wait_ge(s["ot_ps"], it * CH + c + 1)
                for t in range(VT):
                    act.activation(oT[:, t, :], ps[:, CX, t * P:(t + 1) * P], ACT.Copy,
                                   scale=gw[:, t:t + 1]).then_inc(s["oT_ok"], 1)

            on.update(merge2=merge2, qk=qk_, v=v_, gate=gate, scores=scores, values=values, w0=w0, delta=delta,
                      state_out=state_out, out=squares, ks=ks, oT=turn_out, finish=turn_out)
            act.wait_ge(s["c_ld"], 32)
            run(act, on)

        @block.gpsimd
        def _(pool):
            on = {n: nothing for n in PIECES}

            def norms(st):
                it, m = st
                wait_apart(pool, s["nk"], it + 1, s["passed_pool"])
                pool.tensor_tensor(nrm[:, m], kk[:], half[:], ALU.pow).then_inc(s["nrm_ok"], 1)
                wait_apart(pool, s["qk_ok"], (it + 1) * 2 * PAIRS, s["passed_pool"])
                wait_apart(pool, s["b_ld"], (it + 1) * 32, s["passed_pool"])
                for a in range(PAIRS):
                    pool.tensor_tensor(kqb[:, m, a], qk[:, a, 1], bc(bcb[:, m, a, :], 1, 2), ALU.mult).then_inc(s["kqb_ok"], 1)

            def scores(st, c):
                it, m = st
                us = slice(c * QH, (c + 1) * QH)
                wait_apart(pool, s["b16_c"], it * CH + c + 1, s["passed_pool"])
                pool.affine_select(b16[:, m, us, :], b16[:, m, us, :], [[0, QH], [-1, P]], ALU.not_equal, 1.0, base=0,
                                   channel_multiplier=1).then_inc(s["b16_ok"], 1)
                pool.affine_select(am[:, m, us, 0, :], am[:, m, us, 0, :], [[0, QH], [-1, P]], ALU.not_equal, 1.0, base=0,
                                   channel_multiplier=1).then_inc(s["ia_ok"], 1)

            def scale(st, c):
                it, m = st
                wait_apart(pool, s["vo_ok"], it * CH + c + 1, s["passed_pool"])
                pool.tensor_tensor(fo[:], vo[:], nhalf[:], ALU.pow).then_inc(s["fo_ok"], 1)

            on.update(norms=norms, scores=scores, out=scale, state_out=lambda st: scale(st, 0))
            pool.memset(half[:], 0.5).then_inc(s["set_ok"], 1)
            pool.memset(nhalf[:], -0.5).then_inc(s["set_ok"], 1)
            pool.memset(vo[:], 1.0).then_inc(s["set_ok"], 1)
            pool.wait_ge(s["set_ok"], 6)
            run(pool, on)



def experts(nc, A, mem, scr):
    with ExitStack() as ctx:
        sb = lambda name, shape, dt=F32: ctx.enter_context(nc.sbuf_tensor("ex_" + name, shape, dt))
        sem = lambda name: ctx.enter_context(nc.semaphore("ex_" + name))
        ps = ctx.enter_context(nc.psum_tensor("ex_ps", [P, 8, 512], F32))
        W1 = sb("W1", [P, KT, INTER])
        W3 = sb("W3", [P, KT, INTER])
        W2 = sb("W2", [P, MT, D])
        w2c = sb("w2c", [P, KT])
        gate_w = sb("gate_w", [P, KT, E])
        ew1 = sb("ew1", [P, KT, E, HID])
        eb1 = sb("eb1", [P, E])
        ew2 = sb("ew2", [P, E, D])
        b2 = sb("b2", [E + 1, D])
        sw1 = sb("sw1", [P, KT, SH])
        sb1 = sb("sb1", [P, SH // P])
        sw2 = sb("sw2", [P, SH // P, D])
        modb = sb("modb", [P, 2, 4, D])
        xg = sb("xg", [P, GT, D])
        x2 = sb("x2", [P, GT, D])
        hn = sb("hn", [P, GT, D])
        sq = sb("sq", [P, GT, D])
        ss, ms, rr, nh, var, rstd = (sb(n, [P, GT]) for n in ("ss", "ms", "rr", "nh", "var", "rstd"))
        st = sb("st", [P, GT, 6])
        mv = sb("mv", [P, GT, 2])
        fT = sb("fT", [P, KT, GTOK])
        s1 = sb("s1", [P, 2, GTOK])
        gT = sb("gT", [P, MT, GTOK])
        lg = sb("lg", [P, GT, E])
        top = sb("top", [P, GT, E])
        idx = sb("idx", [P, GT, E], U32)
        idf = sb("idf", [P, GT, 2])
        dl = sb("dl", [P, GT])
        ed = sb("ed", [P, GT])
        pr = sb("pr", [P, GT, 2])
        g2 = sb("g2", [P, GT, E])
        gates = sb("gates", [P, GT, 16])
        gT9 = sb("gT9", [E + 1, GTOK])
        shT = sb("shT", [P, SH // P, GTOK])
        he = sb("he", [P, 2, GTOK])
        yo = sb("yo", [P, GT, D])

        names = """ld x_ld mod_ld out_st set_ok ss_ok ms_ok rr_ok hn_ok tr_ps fT_ok h1_ps s1_ok gT_ok o2_ps x2_ok
            var_ok rstd_ok lg_ps dl_ok ed_ok gates_ok gt_ps gt9_ok sh_ps shT_ok he_ps he_ok y0_ps y0_ok e_ps e_ok out_ok
            chain passed passed_pool passed_sp""".split()
        s = {n: sem(n) for n in names}
        const = mem["const"]
        ident = const[:, C_ID:C_ID + P]
        acc = mem["acc"]
        SLOTS = SH // P
        LDS = 15

        block = ctx.enter_context(nc.Block())

        @block.sync
        def _(sp):
            k_of = lambda ap: ap.rearrange("(k p) n -> p k n", k=KT)
            full = (INTER // P) * P
            loads = [(W1[:], k_of(A["W1"])), (W3[:], k_of(A["W3"])),
                     (W2[:, 0:MT - 1, :], A["W2"][0:full, :].rearrange("(t p) n -> p t n", p=P)),
                     (W2[0:INTER - full, MT - 1, :], A["W2"][full:INTER, :]),
                     (w2c[:], A["rms2_w"]),
                     (gate_w[:], k_of(A["gate_w"]))]
            for k in range(KT):
                loads.append((ew1[:, k], A["w1"][:, k * P:(k + 1) * P, :].rearrange("e p h -> p e h")))
            loads += [(eb1[:], A["b1"]), (ew2[:], A["w2"].rearrange("e h d -> h e d")),
                      (b2[0:E, :], A["b2"]), (b2[E:E + 1, :], A["shared_b2"].rearrange("(a d) -> a d", a=1)),
                      (sw1[:], k_of(A["shared_w1"])), (sb1[:], A["shared_b1"]),
                      (sw2[:], A["shared_w2"].rearrange("(t p) d -> p t d", p=P))]
            assert len(loads) == LDS
            for dst, src in loads:
                sp.dma_start(dst, src).then_inc(s["ld"], 16)
            x_v = A["x"].rearrange("b (c p) d -> p (b c) d", p=P)
            o_v = A["out"].rearrange("b (c p) d -> p (b c) d", p=P)
            def turn(g):
                wait_apart(sp, s["out_ok"], g, s["passed_sp"])
                sp.dma_start(modb[:], scr["mod"][bass.ds(g * 2, 2), 2 * D:6 * D].rearrange("b (n d) -> b n d", n=4)
                             .partition_broadcast(P)).then_inc(s["mod_ld"], 16)
                sp.dma_start(xg[:], x_v[:, bass.ts(g, GT), :]).then_inc(s["x_ld"], 16)
                wait_apart(sp, s["out_ok"], g + 1, s["passed_sp"])
                sp.dma_start(o_v[:, bass.ts(g, GT), :], yo[:]).then_inc(s["out_st"], 16)

            groups(sp, turn)
            sp.wait_ge(s["out_st"], 16 * GROUPS)

        @block.tensor
        def _(pe):
            pe.wait_ge(s["ld"], 16 * LDS)
            def turn(g):
                def transposes(n):
                    pe.wait_ge(s["hn_ok"], (g * 2 + n + 1) * GT)
                    for k in range(KT):
                        for j in range(GT):
                            last = pe.transpose(ps[:, k, j * P:(j + 1) * P], hn[:, j, k * P:(k + 1) * P], ident)
                        last.then_inc(s["tr_ps"], 1)
                    pe.wait_ge(s["fT_ok"], (g * 2 + n + 1) * KT)

                wait(pe, s["e_ok"], g * E * GT)
                transposes(0)
                for m in range(MT):
                    M = min(P, INTER - m * P)
                    if m >= 2:
                        pe.wait_ge(s["gT_ok"], g * MT + m - 1)
                    else:
                        wait(pe, s["he_ok"], g * E)
                    for n, wt in enumerate((W1, W3)):
                        for k in range(KT):
                            last = pe.matmul(ps[0:M, 2 + 2 * (m % 2) + n, :], wt[:, k, m * P:m * P + M], fT[:, k, :],
                                             start=(k == 0), stop=(k == KT - 1))
                        last.then_inc(s["h1_ps"], 1)
                pe.wait_ge(s["gT_ok"], (g + 1) * MT)
                wait(pe, s["y0_ok"], g)
                for j in range(GT):
                    for m in range(MT):
                        M = min(P, INTER - m * P)
                        last = pe.matmul(ps[:, 6 + j // 2, (j % 2) * D:(j % 2 + 1) * D], gT[0:M, m, j * P:(j + 1) * P],
                                         W2[0:M, m, :], start=(m == 0), stop=(m == MT - 1))
                last.then_inc(s["o2_ps"], 1)
                transposes(1)
                for j in range(GT):
                    for k in range(KT):
                        last = pe.matmul(ps[:, 2, j * E:(j + 1) * E], fT[:, k, j * P:(j + 1) * P], gate_w[:, k, :],
                                         start=(k == 0), stop=(k == KT - 1))
                last.then_inc(s["lg_ps"], 1)
                for n in range(SLOTS):
                    for k in range(KT):
                        last = pe.matmul(ps[:, 4 + n, :], sw1[:, k, n * P:(n + 1) * P], fT[:, k, :],
                                         start=(k == 0), stop=(k == KT - 1))
                    last.then_inc(s["sh_ps"], 1)
                pe.wait_ge(s["gates_ok"], g + 1)
                for j in range(GT):
                    last = pe.transpose(ps[0:E + 1, 3, j * P:(j + 1) * P], gates[:, j, 0:E + 1], ident)
                last.then_inc(s["gt_ps"], 1)

                def hidden(e):
                    if e < 2:
                        pe.wait_ge(s["shT_ok"], g * SLOTS + e + 1)
                    else:
                        pe.wait_ge(s["he_ok"], g * E + e - 1)
                    for k in range(KT):
                        last = pe.matmul(ps[:, 4 + e % 2, :], ew1[:, k, e, :], fT[:, k, :], start=(k == 0),
                                         stop=(k == KT - 1))
                    last.then_inc(s["he_ps"], 1)

                hidden(0)
                pe.wait_ge(s["shT_ok"], (g + 1) * SLOTS)
                pe.wait_ge(s["gt9_ok"], g + 1)
                pe.wait_ge(s["x2_ok"], g + 1)
                for j in range(GT):
                    out = ps[:, 6 + j // 2, (j % 2) * D:(j % 2 + 1) * D]
                    for n in range(SLOTS):
                        pe.matmul(out, shT[:, n, j * P:(j + 1) * P], sw2[:, n, :], start=(n == 0), stop=False)
                    last = pe.matmul(out, gT9[:, j * P:(j + 1) * P], b2[:], start=False, stop=True)
                last.then_inc(s["y0_ps"], 1)
                for e in range(E):
                    if e + 1 < E:
                        hidden(e + 1)
                    pe.wait_ge(s["he_ok"], g * E + e + 1)
                    if e >= 2:
                        pe.wait_ge(s["e_ok"], (g * E + e - 1) * GT)
                    for j in range(GT):
                        last = pe.matmul(ps[:, 2 * (e % 2) + j // 2, (j % 2) * D:(j % 2 + 1) * D],
                                         he[:, e % 2, j * P:(j + 1) * P], ew2[:, e, :], start=True, stop=True)
                    last.then_inc(s["e_ps"], 1)

            groups(pe, turn)

        @block.gpsimd
        def _(pool):
            pool.memset(nh[:], -0.5).then_inc(s["set_ok"], 1)
            pool.wait_ge(s["set_ok"], 1)
            def turn(g):
                wait_apart(pool, s["ms_ok"], g + 1, s["passed_pool"])
                pool.tensor_tensor(rr[:], ms[:], nh[:], ALU.pow).then_inc(s["rr_ok"], 1)
                wait_apart(pool, s["var_ok"], g + 1, s["passed_pool"])
                pool.tensor_tensor(rstd[:], var[:], nh[:], ALU.pow).then_inc(s["rstd_ok"], 1)

            groups(pool, turn)

        @block.scalar
        def _(act):
            act.wait_ge(s["ld"], 16 * LDS)
            def turn(g):
                wait(act, s["ms_ok"], g)
                for j in range(GT):
                    act.activation(sq[:, j, :], acc[:, g * GT + j, :], ACT.Square, accum_out=ss[:, j:j + 1]).then_inc(s["ss_ok"], 1)
                for k in range(KT):
                    act.wait_ge(s["tr_ps"], g * 2 * KT + k + 1)
                    act.activation(fT[:, k, :], ps[:, k, :], ACT.Copy, scale=w2c[:, k:k + 1]).then_inc(s["fT_ok"], 1)
                for m in range(MT):
                    M = min(P, INTER - m * P)
                    act.wait_ge(s["h1_ps"], (g * MT + m) * 2 + 1)
                    if m >= 2:
                        act.wait_ge(s["gT_ok"], g * MT + m - 1)
                    act.activation(s1[0:M, m % 2, :], ps[0:M, 2 + 2 * (m % 2), :], ACT.Silu).then_inc(s["s1_ok"], 1)
                for k in range(KT):
                    act.wait_ge(s["tr_ps"], g * 2 * KT + KT + k + 1)
                    act.copy(fT[:, k, :], ps[:, k, :]).then_inc(s["fT_ok"], 1)
                act.wait_ge(s["dl_ok"], g + 1)
                act.activation(ed[:], dl[:], ACT.Exp).then_inc(s["ed_ok"], 1)
                for n in range(SLOTS):
                    act.wait_ge(s["sh_ps"], g * SLOTS + n + 1)
                    act.activation(shT[:, n, :], ps[:, 4 + n, :], ACT.Gelu, bias=sb1[:, n:n + 1]).then_inc(s["shT_ok"], 1)
                act.wait_ge(s["gt_ps"], g + 1)
                act.copy(gT9[:], ps[0:E + 1, 3, :]).then_inc(s["gt9_ok"], 1)
                for e in range(E):
                    act.wait_ge(s["he_ps"], g * E + e + 1)
                    if e >= 2:
                        act.wait_ge(s["e_ps"], g * E + e - 1)
                    act.activation(he[:, e % 2, :], ps[:, 4 + e % 2, :], ACT.Gelu, bias=eb1[:, e:e + 1]).then_inc(s["he_ok"], 1)

            groups(act, turn)

        @block.vector
        def _(v):
            v.memset(gates[:], 1.0)
            def turn(g):
                c = Chain(v, s["chain"], g, CHAIN_EX)
                v.wait_ge(s["ss_ok"], (g + 1) * GT)
                v.tensor_scalar(ms[:], ss[:], 1.0 / D, RMS_EPS, ALU.mult, ALU.add).then_inc(s["ms_ok"], 1)
                v.wait_ge(s["rr_ok"], g + 1)
                for j in range(GT):
                    v.tensor_scalar(hn[:, j, :], acc[:, g * GT + j, :], rr[:, j:j + 1], None, ALU.mult).then_inc(s["hn_ok"], 1)
                for m in range(MT):
                    M = min(P, INTER - m * P)
                    v.wait_ge(s["s1_ok"], g * MT + m + 1)
                    v.wait_ge(s["h1_ps"], (g * MT + m) * 2 + 2)
                    v.tensor_tensor(gT[0:M, m, :], s1[0:M, m % 2, :], ps[0:M, 3 + 2 * (m % 2), :], ALU.mult).then_inc(s["gT_ok"], 1)
                v.wait_ge(s["o2_ps"], g + 1)
                for n in range(2):
                    v2 = x2[:, 2 * n:2 * n + 2, :]
                    c.add(v.tensor_tensor(v2, acc[:, bass.ds(g * GT + 2 * n, 2), :],
                                          ps[:, 6 + n, :].rearrange("p (j d) -> p j d", j=2), ALU.add))
                c.sync()
                v.wait_ge(s["mod_ld"], (g + 1) * 16)
                for n in range(2):
                    v2 = x2[:, 2 * n:2 * n + 2, :]
                    c.add(v.tensor_tensor(v2, v2, bc(modb[:, n, 0, :], 1, 2), ALU.mult))
                c.sync()
                v.wait_ge(s["x_ld"], (g + 1) * 16)
                v.tensor_tensor(x2[:], x2[:], xg[:], ALU.add).then_inc(s["x2_ok"], 1)
                v.wait_ge(s["x2_ok"], g + 1)
                for j in range(GT):
                    c.add(v.bn_stats(st[:, j, :], x2[:, j, :]))
                c.sync_apart(s["passed"])
                for j in range(GT):
                    c.add(v.bn_aggr(mv[:, j, :], st[:, j, :]))
                c.sync()
                v.tensor_scalar(var[:], mv[:, :, 1], RMS_EPS, None, ALU.add).then_inc(s["var_ok"], 1)
                v.wait_ge(s["rstd_ok"], g + 1)
                for j in range(GT):
                    c.add(v.tensor_scalar(hn[:, j, :], x2[:, j, :], mv[:, j, 0:1], rstd[:, j:j + 1], ALU.subtract, ALU.mult))
                c.sync()
                for n in range(2):
                    v2 = hn[:, 2 * n:2 * n + 2, :]
                    c.add(v.tensor_tensor(v2, v2, bc(modb[:, n, 2, :], 1, 2), ALU.mult))
                c.sync()
                for n in range(2):
                    v2 = hn[:, 2 * n:2 * n + 2, :]
                    v.tensor_tensor(v2, v2, bc(modb[:, n, 1, :], 1, 2), ALU.add).then_inc(s["hn_ok"], 2)
                v.wait_ge(s["lg_ps"], g + 1)
                c.add(v.tensor_copy(lg[:], ps[:, 2, 0:GT * E].rearrange("p (j e) -> p j e", j=GT)))
                c.sync_apart(s["passed"])
                for j in range(GT):
                    c.add(v.max(top[:, j, :], lg[:, j, :]))
                c.sync()
                v.tensor_tensor(dl[:], top[:, :, 1], top[:, :, 0], ALU.subtract).then_inc(s["dl_ok"], 1)
                for j in range(GT):
                    c.add(v.max_index(idx[:, j, :], top[:, j, :], lg[:, j, :]))
                c.sync()
                c.link(v.tensor_copy(idf[:], idx[:, :, 0:2]))
                v.wait_ge(s["ed_ok"], g + 1)
                c.link(v.tensor_scalar(dl[:], ed[:], 1.0, None, ALU.add))
                c.link(v.reciprocal(pr[:, :, 0], dl[:]))
                c.link(v.tensor_tensor(pr[:, :, 1], pr[:, :, 0], ed[:], ALU.mult))
                for j in range(GT):
                    for n, dst in ((0, gates[:, j, 0:E]), (1, g2[:, j, :])):
                        c.add(v.tensor_scalar(dst, const[:, C_IOTA:C_IOTA + E], idf[:, j, n:n + 1], pr[:, j, n:n + 1],
                                              ALU.is_equal, ALU.mult))
                c.sync()
                v.tensor_tensor(gates[:, :, 0:E], gates[:, :, 0:E], g2[:], ALU.add).then_inc(s["gates_ok"], 1)
                v.wait_ge(s["y0_ps"], g + 1)
                wait(v, s["out_st"], g * 16)
                v.tensor_copy(yo[:].rearrange("p (n j) d -> p n (j d)", n=2), ps[:, 6:8, :]).then_inc(s["y0_ok"], 1)
                v.wait_ge(s["y0_ok"], g + 1)
                for e in range(E):
                    v.wait_ge(s["e_ps"], g * E + e + 1)
                    if e:
                        v.wait_ge(s["e_ok"], (g * E + e) * GT)
                    for j in range(GT):
                        v.scalar_tensor_tensor(yo[:, j, :], ps[:, 2 * (e % 2) + j // 2, (j % 2) * D:(j % 2 + 1) * D],
                                               gates[:, j, e:e + 1], yo[:, j, :], ALU.mult, ALU.add).then_inc(s["e_ok"], 1)
                v.wait_ge(s["e_ok"], (g + 1) * E * GT)
                for n in range(2):
                    v2 = yo[:, 2 * n:2 * n + 2, :]
                    c.add(v.tensor_tensor(v2, v2, bc(modb[:, n, 3, :], 1, 2), ALU.mult))
                c.sync()
                v.tensor_tensor(yo[:], yo[:], x2[:], ALU.add).then_inc(s["out_ok"], 1)
                c.close()

            groups(v, turn)


CHAIN_EX = 41


def adaln_block(nc, A):
    with ExitStack() as ctx:
        sb = lambda name, shape, dt=F32: ctx.enter_context(nc.sbuf_tensor(name, shape, dt))
        mem = {
            "const": sb("const", [P, C_COLS]),
            "id16": sb("id16", [P, P], BF16),
            "mask": sb("mask", [P, LEVELS, P], BF16),
            "acc": sb("acc", [P, TILES, D]),
            "hT": sb("hT", [P, KT, B * T]),
            "beta": sb("beta", [P, STEPS, U]),
        }
        scr = {
            "mod": nc.dram_tensor("scr_mod", (B, 6 * D), F32, kind="Internal").ap(),
            "a": nc.dram_tensor("scr_a", (B, H, T), F32, kind="Internal").ap(),
            "b": nc.dram_tensor("scr_b", (B, H, P), F32, kind="Internal").ap(),
        }
        prepare(nc, A, mem, scr)
        delta_rule(nc, A, mem, scr)
        experts(nc, A, mem, scr)


def constants():
    import numpy as np

    c = np.zeros((P, C_COLS), np.float32)
    i = np.arange(P)
    c[:, C_ID:C_ID + P] = np.eye(P)
    for l in range(LEVELS):
        size = 1 << l
        same = i[:, None] // (2 * size) == i[None, :] // (2 * size)
        other = i[:, None] // size != i[None, :] // size
        c[:, C_MASK + l * P:C_MASK + (l + 1) * P] = (same & other) | (i[:, None] == i[None, :])
    c[0:64, C_HEAD] = 1.0
    c[64:128, C_HEAD + 1] = 1.0
    c[:, C_IOTA:C_IOTA + E] = np.arange(E)
    return c


_ATTN = ["x", "rms1_w", "rms2_w", "Wq", "Wk", "Wv", "Wa", "Wb", "Wg", "dt_bias", "A_log", "conv_q_w", "conv_k_w",
         "conv_v_w", "gnorm_w", "Wo", "W1", "W3", "W2"]
_FFN = ["gate_w", "w1", "b1", "w2", "b2", "shared_w1", "shared_b1", "shared_w2", "shared_b2"]


def kernel(**inputs):
    import numpy as np
    import concourse.bacc as bacc
    from concourse.bass_utils import run_bass_kernel_spmd

    nc = bacc.Bacc("TRN2", target_bir_lowering=False, num_devices=1)
    named = {n: "L0_attn_" + n for n in _ATTN} | {n: "L0_ffn_" + n for n in _FFN} | {"c": "L0_c", "wmod": "L0_wmod"}
    host = {n: np.asarray(inputs[full]) for n, full in named.items()}
    host["c"] = host["c"].T.reshape(KT, P, B).transpose(1, 0, 2)
    host["b1"] = host["b1"].T
    for n in ("rms1_w", "rms2_w", "shared_b1"):
        host[n] = host[n].reshape(-1, P).T
    host["gnorm_w"] = np.concatenate([host["gnorm_w"]] * QH).reshape(VT, P).T
    host = {n: np.ascontiguousarray(a) for n, a in host.items()}
    host["consts"] = constants()
    A = {n: nc.dram_tensor("in_" + n, a.shape, mybir.dt.from_np(a.dtype), kind="ExternalInput").ap()
         for n, a in host.items()}
    A["out"] = nc.dram_tensor("out", (B, T, D), F32, kind="ExternalOutput").ap()
    adaln_block(nc, A)
    r = run_bass_kernel_spmd(nc, [{"in_" + n: a for n, a in host.items()}], core_ids=[0])
    return r.results[0]["out"]
```

```python
from contextlib import ExitStack

import concourse.bass as bass
from concourse import mybir

F32 = mybir.dt.float32
BF16 = mybir.dt.bfloat16
U32 = mybir.dt.uint32
ALU = mybir.AluOpType
ACT = mybir.ActivationFunctionType
AX_X = mybir.AxisListType.X

B, T, D = 8, 256, 256
H, DK, DV = 32, 48, 96
TAPS = 4
INTER = 704
E, HID = 8, 128
SH = 2 * HID
P = 128
KT = D // P
CH = T // P
QH = 4
NQ = H // QH
PAIRS = QH // 2
QV = QH * DV
VT = QV // P
STEPS = NQ * B
U = CH * QH
LEVELS = 7
REFINE = 2
NB = 3
TILES = B * T // P
GT = 4
GROUPS = TILES // GT
GTOK = GT * P
MT = (INTER + P - 1) // P
RMS_EPS = 1e-5
L2_EPS = 1e-6
ATANH = [1.0 / (2 * k + 1) for k in range(9)]

C_ID, C_MASK, C_HEAD, C_IOTA = 0, P, P * (1 + LEVELS), P * (1 + LEVELS) + 2
C_COLS = C_IOTA + E


def wait(eng, sem, value):
    if not (isinstance(value, int) and value <= 0):
        eng.wait_ge(sem, value)


def wait_apart(eng, sem, value, passed):
    if isinstance(value, int):
        wait(eng, sem, value)
    else:
        eng.wait_ge(sem, value)
        eng.sem_inc(passed, 1)


def groups(eng, turn):
    turn(0)
    with eng.Fori(1, GROUPS) as g:
        turn(g)


class Chain:

    def __init__(self, eng, sem, turn=0, per=0):
        self.eng, self.sem, self.base, self.per, self.n = eng, sem, turn * per, per, 0

    def link(self, ins):
        self.n += 1
        ins.then_inc(self.sem, 1)
        self.eng.wait_ge(self.sem, self.base + self.n)

    def add(self, ins):
        self.n += 1
        ins.then_inc(self.sem, 1)

    def sync(self):
        self.eng.wait_ge(self.sem, self.base + self.n)

    def sync_apart(self, passed):
        wait_apart(self.eng, self.sem, self.base + self.n, passed)

    def close(self):
        assert self.n == self.per, (self.n, self.per)


def bc(ap, axis, n):
    v = ap.unsqueeze(axis)
    shape = list(v.shape)
    shape[axis] = n
    return v.broadcast_to(shape)


def prepare(nc, A, mem, scr):
    with ExitStack() as ctx:
        sb = lambda name, shape, dt=F32: ctx.enter_context(nc.sbuf_tensor("p1_" + name, shape, dt))
        sem = lambda name: ctx.enter_context(nc.semaphore("p1_" + name))
        ps = ctx.enter_context(nc.psum_tensor("p1_ps", [P, 8, 512], F32))
        x1 = sb("x1", [P, TILES, D])
        modb = sb("modb", [P, B, 2 * D])
        ct = sb("ct", [P, KT, B])
        cs = sb("cs", [P, KT, B])
        wmod = sb("wmod", [P, KT, 6 * D])
        mod = sb("mod", [B, 6 * D])
        sgn = sb("sgn", [B, 6 * D])
        wab = sb("wab", [P, KT, 2 * H])
        w1c = sb("w1c", [P, KT])
        dtb = sb("dtb", [P, 1])
        alog = sb("alog", [P, 1])
        ea = sb("ea", [P, 1])
        st = sb("st", [P, GT, 6])
        mv = sb("mv", [P, GT, 2])
        var = sb("var", [P, GT])
        rstd = sb("rstd", [P, GT])
        ss = sb("ss", [P, GT])
        ms = sb("ms", [P, GT])
        rr = sb("rr", [P, GT])
        nh = sb("nh", [P, GT])
        sq = sb("sq", [P, GT, D])
        hn = sb("hn", [P, GT, D])
        tmp = {n: sb("t_" + n, [P, GTOK]) for n in ("z", "u", "m", "zz", "z2", "p", "q", "a", "b", "bc", "zero", "zb")}

        ld, ldx, mod_st, modb_ld, scr_st = (sem(n) for n in ("ld", "ldx", "mod_st", "modb_ld", "scr_st"))
        c_silu, mod_ps, mod_ok = (sem(n) for n in ("c_silu", "mod_ps", "mod_ok"))
        dve, half_ok = (sem(n) for n in ("dve", "half_ok"))
        var_ok, rstd_ok, h0_ok, ss_ok, ms_ok, rr_ok, hn_ok, tr_ps, ht_ok = (
            sem(n) for n in ("var_ok", "rstd_ok", "h0_ok", "ss_ok", "ms_ok", "rr_ok", "hn_ok", "tr_ps", "ht_ok"))
        z_ps, absz_ok, u_ok, sp_ok, a_ok, eb_ok, beta_ok, bt_ps, bcum_ok = (
            sem(n) for n in ("z_ps", "absz_ok", "u_ok", "sp_ok", "a_ok", "eb_ok", "beta_ok", "bt_ps", "bcum_ok"))
        acts, done, late, passed, passed_pool = (sem(n) for n in ("acts", "done", "late", "passed", "passed_pool"))
        NLD = 1 + 1 + 2 + 1 + 2 * GROUPS + 1

        block = ctx.enter_context(nc.Block())

        @block.sync
        def _(sp):
            sp.dma_start(mem["const"][:], A["consts"]).then_inc(ld, 16)
            sp.dma_start(ct[:], A["c"]).then_inc(ld, 16)
            sp.dma_start(wmod[:], A["wmod"].rearrange("(k p) n -> p k n", k=KT)).then_inc(ld, 16)
            sp.dma_start(wab[:, :, 0:H], A["Wa"].rearrange("(k p) n -> p k n", k=KT)).then_inc(ld, 16)
            sp.dma_start(wab[:, :, H:2 * H], A["Wb"].rearrange("(k p) n -> p k n", k=KT)).then_inc(ld, 16)
            sp.dma_start(w1c[:], A["rms1_w"]).then_inc(ld, 16)
            for g in range(GROUPS):
                sp.dma_start(dtb[H * g:H * (g + 1), :], A["dt_bias"].rearrange("(h a) -> h a", a=1)).then_inc(ld, 16)
                sp.dma_start(alog[H * g:H * (g + 1), :], A["A_log"].rearrange("(h a) -> h a", a=1)).then_inc(ld, 16)
            for g in range(GROUPS):
                sp.dma_start(x1[:, g * GT:(g + 1) * GT, :],
                             A["x"].rearrange("b (c p) d -> p (b c) d", p=P)[:, g * GT:(g + 1) * GT, :]).then_inc(ldx, 16)
            sp.wait_ge(mod_ok, 2)
            sp.dma_start(scr["mod"], mod[:]).then_inc(mod_st, 16)
            sp.wait_ge(mod_st, 16)
            sp.dma_start(modb[:], scr["mod"][:, 0:2 * D].partition_broadcast(P)).then_inc(modb_ld, 16)
            sp.wait_ge(a_ok, 1)
            for g in range(GROUPS):
                sp.dma_start(scr["a"][2 * g:2 * g + 2].rearrange("b h t -> h b t"),
                             tmp["a"][H * g:H * (g + 1), :].rearrange("h (b t) -> h b t", b=2)).then_inc(scr_st, 16)
            sp.wait_ge(bcum_ok, CH * 2)
            for g in range(GROUPS):
                sp.dma_start(scr["b"][2 * g:2 * g + 2].rearrange("b h t -> h b t"),
                             tmp["bc"][H * g:H * (g + 1), :].rearrange("h (b c t) -> h b c t", b=2, c=CH)[:, :, 1, :]
                             ).then_inc(scr_st, 16)
            sp.wait_ge(scr_st, 2 * GROUPS * 16)

        @block.tensor
        def _(pe):
            pe.wait_ge(ld, 16 * NLD + 0)
            pe.wait_ge(c_silu, 1)
            for n in range(3):
                for k in range(KT):
                    last = pe.matmul(ps[0:B, n, :], cs[:, k, :], wmod[:, k, n * 512:(n + 1) * 512],
                                     start=(k == 0), stop=(k == KT - 1))
            last.then_inc(mod_ps, 1)
            def turn(g):
                pe.wait_ge(hn_ok, (g + 1) * GT)
                wait(pe, ht_ok, g * KT)
                for k in range(KT):
                    for j in range(GT):
                        last = pe.transpose(ps[:, 3 + k, j * P:(j + 1) * P], hn[:, j, k * P:(k + 1) * P],
                                            mem["const"][:, C_ID:C_ID + P])
                    last.then_inc(tr_ps, 1)

            groups(pe, turn)
            pe.wait_ge(ht_ok, GROUPS * KT)
            pe.wait_ge(mod_ok, 2)
            for w in range(2):
                for g in range(GROUPS):
                    for k in range(KT):
                        last = pe.matmul(ps[H * g:H * (g + 1), w, :], wab[:, k, H * w:H * (w + 1)],
                                         mem["hT"][:, k, g * GTOK:(g + 1) * GTOK], start=(k == 0), stop=(k == KT - 1))
                last.then_inc(z_ps, 1)
            pe.wait_ge(beta_ok, 1)
            for j in range(GT):
                last = pe.transpose(ps[:, 2, j * P:(j + 1) * P], tmp["b"][:, j * P:(j + 1) * P],
                                    mem["const"][:, C_ID:C_ID + P])
            last.then_inc(bt_ps, 1)

        @block.gpsimd
        def _(pool):
            pool.memset(nh[:], -0.5).then_inc(half_ok, 1)
            pool.wait_ge(half_ok, 1)
            def turn(g):
                wait_apart(pool, var_ok, g + 1, passed_pool)
                pool.tensor_tensor(rstd[:], var[:], nh[:], ALU.pow).then_inc(rstd_ok, 1)
                wait_apart(pool, ms_ok, g + 1, passed_pool)
                pool.tensor_tensor(rr[:], ms[:], nh[:], ALU.pow).then_inc(rr_ok, 1)

            groups(pool, turn)

        @block.scalar
        def _(act):
            act.wait_ge(ld, 16 * NLD)
            act.activation(cs[:], ct[:], ACT.Silu).then_inc(c_silu, 1)
            def turn(g):
                act.wait_ge(h0_ok, (g + 1) * 2)
                for j in range(GT):
                    act.activation(sq[:, j, :], mem["acc"][:, g * GT + j, :], ACT.Square,
                                   accum_out=ss[:, j:j + 1]).then_inc(ss_ok, 1)
                for k in range(KT):
                    act.wait_ge(tr_ps, g * KT + k + 1)
                    act.activation(mem["hT"][:, k, bass.ts(g, GTOK)], ps[:, 3 + k, :], ACT.Copy,
                                   scale=w1c[:, k:k + 1]).then_inc(ht_ok, 1)

            groups(act, turn)
            act.activation(ea[:], alog[:], ACT.Exp).then_inc(acts, 1)
            act.wait_ge(absz_ok, 1)
            act.activation(tmp["u"][:], tmp["p"][:], ACT.Exp, scale=-1.0).then_inc(u_ok, 1)
            act.wait_ge(z_ps, 2)
            act.activation(tmp["zb"][:], ps[:, 1, :], ACT.Exp, scale=-1.0).then_inc(eb_ok, 1)
            act.wait_ge(sp_ok, 1)
            act.activation(tmp["a"][:], tmp["z"][:], ACT.Exp, scale=-1.0).then_inc(a_ok, 1)

        @block.vector
        def _(v):
            c = Chain(v, dve)
            v.wait_ge(ld, 16 * NLD)
            const = mem["const"]
            v.memset(tmp["zero"][:], 0.0)
            v.tensor_copy(mem["id16"][:], const[:, C_ID:C_ID + P])
            v.tensor_copy(mem["mask"][:], const[:, C_MASK:C_MASK + LEVELS * P].rearrange("p (l n) -> p l n", l=LEVELS))
            v.wait_ge(mod_ps, 1)
            c.link(v.tensor_copy(mod[:], ps[0:B, 0:3, :].rearrange("b n m -> b (n m)")))
            for n in (1, 4):
                c.add(v.tensor_scalar(mod[:, n * D:(n + 1) * D], mod[:, n * D:(n + 1) * D], 1.0, None, ALU.add))
            for n in (2, 5):
                c.add(v.tensor_scalar(sgn[:, n * D:(n + 1) * D], mod[:, n * D:(n + 1) * D], 0.0, 2.0, ALU.is_ge, ALU.mult))
            c.sync()
            for n in (2, 5):
                ns = slice(n * D, (n + 1) * D)
                c.link(v.tensor_scalar(sgn[:, ns], sgn[:, ns], -1.0, None, ALU.add))
                c.link(v.tensor_tensor(mod[:, ns], mod[:, ns], sgn[:, ns], ALU.mult))
                v.scalar_tensor_tensor(mod[:, ns], mod[:, ns], 0.25, sgn[:, ns], ALU.max, ALU.mult).then_inc(mod_ok, 1)
            v.wait_ge(modb_ld, 16)
            v.wait_ge(ldx, 16 * GROUPS)
            def turn(g):
                c = Chain(v, done, g, 3 * GT + 2)
                acc = mem["acc"]
                for j in range(GT):
                    c.add(v.bn_stats(st[:, j, :], x1[:, g * GT + j, :]))
                c.sync_apart(passed)
                for j in range(GT):
                    c.add(v.bn_aggr(mv[:, j, :], st[:, j, :]))
                c.sync()
                v.tensor_scalar(var[:], mv[:, :, 1], RMS_EPS, None, ALU.add).then_inc(var_ok, 1)
                v.wait_ge(rstd_ok, g + 1)
                for j in range(GT):
                    c.add(v.tensor_scalar(acc[:, g * GT + j, :], x1[:, g * GT + j, :], mv[:, j, 0:1], rstd[:, j:j + 1],
                                          ALU.subtract, ALU.mult))
                c.sync()
                for half, op in ((1, ALU.mult), (0, ALU.add)):
                    for b2 in range(2):
                        v2 = acc[:, bass.ds(g * GT + 2 * b2, 2), :]
                        ins = v.tensor_tensor(v2, v2, bc(modb[:, g * 2 + b2, half * D:(half + 1) * D], 1, 2), op)
                        if half:
                            c.add(ins)
                        else:
                            ins.then_inc(h0_ok, 1)
                    c.sync()
                v.wait_ge(ss_ok, (g + 1) * GT)
                v.tensor_scalar(ms[:], ss[:], 1.0 / D, RMS_EPS, ALU.mult, ALU.add).then_inc(ms_ok, 1)
                v.wait_ge(rr_ok, g + 1)
                wait(v, tr_ps, g * KT)
                for j in range(GT):
                    v.tensor_scalar(hn[:, j, :], acc[:, g * GT + j, :], rr[:, j:j + 1], None, ALU.mult).then_inc(hn_ok, 1)
                c.close()

            groups(v, turn)
            t = tmp
            c = Chain(v, late)
            v.wait_ge(z_ps, 1)
            c.link(v.tensor_scalar(t["z"][:], ps[:, 0, :], dtb[:, 0:1], None, ALU.add))
            v.scalar_tensor_tensor(t["p"][:], t["z"][:], -1.0, t["z"][:], ALU.mult, ALU.max).then_inc(absz_ok, 1)
            c.add(v.tensor_scalar(t["m"][:], t["z"][:], 0.0, None, ALU.max))
            v.wait_ge(u_ok, 1)
            c.link(v.tensor_scalar(t["p"][:], t["u"][:], 2.0, None, ALU.add))
            c.link(v.reciprocal(t["q"][:], t["p"][:]))
            c.link(v.tensor_tensor(t["zz"][:], t["u"][:], t["q"][:], ALU.mult))
            c.link(v.tensor_tensor(t["z2"][:], t["zz"][:], t["zz"][:], ALU.mult))
            c.link(v.tensor_scalar(t["p"][:], t["z2"][:], ATANH[-1], None, ALU.mult))
            for k in range(len(ATANH) - 2, 0, -1):
                c.link(v.scalar_tensor_tensor(t["p"][:], t["p"][:], ATANH[k], t["z2"][:], ALU.add, ALU.mult))
            c.link(v.scalar_tensor_tensor(t["p"][:], t["p"][:], 1.0, t["zz"][:], ALU.add, ALU.mult))
            c.link(v.scalar_tensor_tensor(t["p"][:], t["p"][:], 2.0, t["m"][:], ALU.mult, ALU.add))
            v.wait_ge(acts, 1)
            v.tensor_scalar(t["z"][:], t["p"][:], ea[:, 0:1], None, ALU.mult).then_inc(sp_ok, 1)
            v.wait_ge(eb_ok, 1)
            c.link(v.tensor_scalar(t["q"][:], t["zb"][:], 1.0, None, ALU.add))
            v.reciprocal(t["b"][:], t["q"][:]).then_inc(beta_ok, 1)
            v.wait_ge(a_ok, 1)
            for n in range(2 * CH):
                v.tensor_tensor_scan(t["bc"][:, n * P:(n + 1) * P], t["a"][:, n * P:(n + 1) * P],
                                     t["zero"][:, n * P:(n + 1) * P], 1.0, ALU.mult, ALU.add).then_inc(bcum_ok, 1)
            v.wait_ge(bt_ps, 1)
            for j in range(GT):
                out = mem["beta"][:].rearrange("p (q g a) (c h) -> p a c g q h", q=NQ, g=GROUPS, c=CH)[:, j // 2, j % 2]
                src = ps[:, 2, j * P:(j + 1) * P].rearrange("p (g q h) -> p g q h", g=GROUPS, q=NQ)
                c.add(v.tensor_copy(out, src))
            c.sync()


def delta_rule(nc, A, mem, scr):
    with ExitStack() as ctx:
        sb = lambda name, shape, dt=F32: ctx.enter_context(nc.sbuf_tensor("dr_" + name, shape, dt))
        sem = lambda name: ctx.enter_context(nc.semaphore("dr_" + name))
        ps = ctx.enter_context(nc.psum_tensor("dr_ps", [P, 8, 512], F32))
        A0, A1, X0, X1, X2, CW, CX, CO = range(8)

        hb = sb("hb", [P, NB, KT, T])
        abc = sb("abc", [P, NB, QH, T])
        bcb = sb("bcb", [P, NB, PAIRS, P])
        wqk = sb("wqk", [P, KT, 2 * PAIRS, P])
        wv = sb("wv", [P, KT, QV])
        wg = sb("wg", [P, KT, QV])
        cw = sb("cw", [P, 2 * PAIRS + VT, TAPS])
        wo = sb("wo", [P, NQ * VT, D])
        gw = sb("gw", [P, VT])
        y = sb("y", [P, 4, T])
        qk = sb("qk", [P, PAIRS, CH, 2, P])
        vT = sb("vT", [P, VT, T])
        sq = sb("sq", [P, 2, PAIRS, T])
        dec = sb("dec", [P, U, P])
        am = sb("am", [P, NB, U, 2, P])
        b16 = sb("b16", [P, NB, U, P], BF16)
        tn = sb("tn", [P, U, P], BF16)
        tt = sb("tt", [P, U, P], BF16)
        w16 = sb("w16", [P, U, P], BF16)
        tf = sb("tf", [P, NB, U, P], BF16)
        rhs = sb("rhs", [P, NB, CH, QV])
        rhs16 = sb("rhs16", [P, NB, CH, QV], BF16)
        kg = sb("kg", [P, NB, QH, 64])
        kqb = sb("kqb", [P, NB, PAIRS, 2, P])
        gs = sb("gs", [P, NB, CH, QV])
        w = sb("w", [P, CH, QV])
        r16 = sb("r16", [P, QV], BF16)
        S = sb("S", [P, PAIRS, 2 * DV])
        og = sb("og", [P, CH, QV])
        oT = sb("oT", [P, VT, P])
        sqo = sb("sqo", [P, QV])
        kk = sb("kk", [P, U])
        rkk = sb("rkk", [P, U])
        gam = sb("gam", [P, NB, U])
        nrm = sb("nrm", [P, NB, U])
        e2 = sb("e2", [P, NB, U])
        cj = sb("cj", [P, QH])
        mso = sb("mso", [P, QH])
        vo = sb("vo", [P, QH])
        fo = sb("fo", [P, QH])
        half = sb("half", [P, U])
        nhalf = sb("nhalf", [P, QH])

        names = """w_ld h_ld a_ld b_ld c_ld set_ok qk_ps v_ps g_ps n_ps kt_ps kk_ps vt_ps
            tap0 tap qk_ok v_ok sq_ok nk rk gam_ok e2_ok nrm_ok cj_ok kg_ok gs_ok dec_ok am_ok b16_c b16_ok ia_ok
            kqb_ok r_ok r16_ok p1 p2 p3 mask_ok tn_ok tt_ok
            w0_ps res_ps d_ps s_ps ks_ps o_ps ot_ps wo_ps w_ok rs_ok S_ok r1_ok r1h_ok sqo_ok mso_ok vo_ok fo_ok
            og_ok oT_ok acc_ok passed_pool passed_sp""".split()
        s = {n: sem(n) for n in names}
        WDMAS = KT * 2 + 2 + 2 * QH + 1
        const, id16, mask = mem["const"], mem["id16"], mem["mask"]
        ident = const[:, C_ID:C_ID + P]
        NT = 2 * PAIRS + VT

        block = ctx.enter_context(nc.Block())

        def steps(eng, turn):
            turn((0, 0), None, None, None)
            turn((1, 1), (0, 0), None, None)
            turn((2, 2), (1, 1), (0, 0), None)
            full = STEPS - 3
            loops = full // NB
            with eng.Fori(0, loops) as i:
                for m in range(NB):
                    d = i * NB + m
                    turn((d + 3, m), (d + 2, (m + 2) % NB), (d + 1, (m + 1) % NB), (d, m))
            for d in range(loops * NB, full):
                turn((d + 3, d % NB), (d + 2, (d + 2) % NB), (d + 1, (d + 1) % NB), (d, d % NB))
            d = full
            turn(None, (d + 2, (d + 2) % NB), (d + 1, (d + 1) % NB), (d, d % NB))
            turn(None, None, (d + 2, (d + 2) % NB), (d + 1, (d + 1) % NB))
            turn(None, None, None, (d + 2, (d + 2) % NB))

        C_AT = {0: [("w0", 0)], 1: [("residual", 0, 0)], 2: [("delta", 0, 0)], 3: [("residual", 0, 1)],
                4: [("delta", 0, 1)], 5: [("state_out",)], 6: [("ks",), ("mean", 0)], 7: [("w0", 1)],
                8: [("residual", 1, 0), ("gated", 0)], 9: [("delta", 1, 0), ("oT", 0)], 10: [("residual", 1, 1), ("wo", 0)],
                11: [("delta", 1, 1), ("acc", 0)], 12: [("out", 1)], 13: [("mean", 1)]}
        D_AT = {0: [("gated", 1)], 1: [("oT", 1)], 3: [("wo", 1)], 4: [("acc", 1)]}
        A_AT = {0: [("qk", 0)], 1: [("taps", 0, 0)], 2: [("taps", 0, 1), ("qk", 1), ("decays", 0)],
                3: [("taps", 1, 0)], 4: [("taps", 1, 1), ("v", 0)], 5: [("taps", 2, 0)],
                6: [("taps", 2, 1), ("norms",), ("v", 1)], 7: [("gains",), ("taps", 3, 0), ("gate", 0)],
                8: [("keys",), ("gate", 1)], 9: [("scores", 0)], 10: [("decayed", 0, 0), ("decayed", 0, 1)],
                11: [("scores", 1), ("decays", 1)], 12: [("decayed", 1, 0), ("values", 0)],
                13: [("decayed", 1, 1), ("round", 0)], 14: [("values", 1)]}
        A_FIRST = {3: [("qk_silu", 0)], 5: [("qk_silu", 1)], 7: [("v_silu", 0)], 8: [("v_silu", 1)],
                   11: [("negate", 0)], 14: [("negate", 1)]}

        def slots(a, b, c, d, on):
            for half in range(2 * LEVELS + 1):
                if b and half:
                    on["merge2"](b, (half - 1) // 2, (half - 1) % 2)
                if b and half < 2 * LEVELS:
                    on["merge1"](b, half // 2, half % 2)
                for st, pieces in ((a, A_FIRST), (c, C_AT), (d, D_AT), (a, A_AT)):
                    for piece in pieces.get(half, []) if st else []:
                        on[piece[0]](st, *piece[1:])

        def run(eng, on):
            steps(eng, lambda a, b, c, d: slots(a, b, c, d, on))

        def nothing(*_):
            return None

        PIECES = ("merge1", "merge2", "w0", "delta", "residual", "ks", "out", "state_out", "mean", "gated", "oT", "wo",
                  "acc", "qk", "qk_silu", "v", "v_silu", "taps", "gate", "norms", "gains", "decays", "keys", "scores", "decayed", "negate",
                  "values", "round")

        @block.sync
        def _(sp):
            sp.dma_start(wo[:], A["Wo"].rearrange("(t p) n -> p t n", p=P)).then_inc(s["c_ld"], 16)
            sp.dma_start(gw[:], A["gnorm_w"]).then_inc(s["c_ld"], 16)

            sp.wait_ge(s["set_ok"], 6)

            def weights(q):
                wait_apart(sp, s["v_ps"], q * B * 2, s["passed_sp"])
                wait_apart(sp, s["g_ps"], q * B * 2, s["passed_sp"])
                wait_apart(sp, s["v_ok"], q * B * VT, s["passed_sp"])
                for k in range(KT):
                    for n, name in enumerate(("Wq", "Wk")):
                        sp.dma_start(wqk[:, k, 2 * n:2 * n + 2, :].rearrange("p a (h d) -> p (a h) d", h=2)[:, :, 0:DK],
                                     A[name][k * P:(k + 1) * P, bass.ds(q * (QH * DK), QH * DK)]
                                     .rearrange("p (h d) -> p h d", d=DK)).then_inc(s["w_ld"], 16)
                for wt, name in ((wv, "Wv"), (wg, "Wg")):
                    sp.dma_start(wt[:], A[name][:, bass.ds(q * QV, QV)].rearrange("(k p) n -> p k n", k=KT)
                                 ).then_inc(s["w_ld"], 16)
                for n, name in enumerate(("conv_q_w", "conv_k_w")):
                    for h in range(QH):
                        sp.dma_start(cw[64 * (h % 2):64 * (h % 2) + DK, 2 * n + h // 2, :],
                                     A[name][bass.ds(q * (QH * DK) + h * DK, DK), :]).then_inc(s["w_ld"], 16)
                sp.dma_start(cw[:, 2 * PAIRS:, :], A["conv_v_w"][bass.ds(q * QV, QV), :].rearrange("(t p) k -> p t k", p=P)
                             ).then_inc(s["w_ld"], 16)

            def batch(q, b):
                it = q * B + b
                m = it % NB
                if not isinstance(it, int) or it >= NB:
                    wait_apart(sp, s["g_ps"], (it - NB + 1) * 2, s["passed_sp"])
                    wait_apart(sp, s["dec_ok"], (it - NB + 1) * U, s["passed_sp"])
                    wait_apart(sp, s["kqb_ok"], (it - NB + 1) * PAIRS, s["passed_sp"])
                wait_apart(sp, s["h_ld"], it * 16, s["passed_sp"])
                wait_apart(sp, s["a_ld"], it * 16, s["passed_sp"])
                wait_apart(sp, s["b_ld"], it * 32, s["passed_sp"])
                sp.dma_start(hb[:, m], mem["hT"][:, :, bass.ts(b, T)]).then_inc(s["h_ld"], 16)
                sp.dma_start(abc[:, m], scr["a"][b, bass.ds(q * QH, QH), :].partition_broadcast(P)).then_inc(s["a_ld"], 16)
                for side in range(2):
                    src = scr["b"][b, bass.ds(q * QH, QH), :].rearrange("(a s) t -> s a t", s=2)[side]
                    sp.dma_start(bcb[64 * side:64 * side + 64, m], src.partition_broadcast(64)).then_inc(s["b_ld"], 16)

            weights(0)
            for b in range(B):
                batch(0, b)
            with sp.Fori(1, NQ) as q:
                weights(q)
                with sp.Fori(0, B) as b:
                    batch(q, b)
            sp.wait_ge(s["acc_ok"], STEPS * CH + 1)

        @block.tensor
        def _(pe):
            on = {n: nothing for n in PIECES}

            def merge1(st, l, g):
                it, m = st
                if l == 0:
                    pe.wait_ge(s["b16_ok"], it * CH + g + 1)
                    if g == 0:
                        wait(pe, s["tt_ok"], (it * LEVELS - 1) * 2 + 1 if not isinstance(it, int) or it else 0)
                else:
                    pe.wait_ge(s["tt_ok"], (it * LEVELS + l - 1) * 2 + g + 1)
                    if l > 1:
                        pe.wait_ge(s["tn_ok"], (it * (LEVELS - 2) + l - 2) * 2 + g + 1)
                for u in range(QH * g, QH * g + QH):
                    last = pe.matmul(ps[:, (X0, X1)[g], (u % QH) * P:(u % QH + 1) * P], b16[:, m, u, :],
                                     id16[:] if l == 0 else tn[:, u, :], start=True, stop=True)
                last.then_inc(s["p1"], 1)

            def merge2(st, l, g):
                it, m = st
                pe.wait_ge(s["mask_ok"], (it * LEVELS + l) * 2 + g + 1)
                if g == 0:
                    wait(pe, s["tt_ok"], (it * LEVELS + l) * 2 if not isinstance(it, int) or it or l else 0)
                middle = 0 < l < LEVELS - 1
                us = range(QH * g, QH * g + QH)
                if middle:
                    for u in us:
                        last = pe.matmul(ps[:, (X2, X1)[g], (u % QH) * P:(u % QH + 1) * P], tt[:, u, :], w16[:, u, :],
                                         start=True, stop=True)
                    last.then_inc(s["p2"], 1)
                    if g == 1:
                        pe.wait_ge(s["tn_ok"], (it * (LEVELS - 2) + l - 1) * 2 + 1)
                wt = tn if l == 0 else w16
                for u in us:
                    last = pe.matmul(ps[:, (X0, X2)[g], (u % QH) * P:(u % QH + 1) * P], wt[:, u, :],
                                     id16[:] if l == 0 else tt[:, u, :], start=True, stop=True)
                last.then_inc(s["p3"], 1)

            def project(bank, off, wt, m):
                for k in range(KT):
                    last = pe.matmul(ps[:, bank, off:off + T], wt(k), hb[:, m, k, :], start=(k == 0), stop=(k == KT - 1))
                return last

            def qk_(st, n):
                it, m = st
                if n == 0:
                    pe.wait_ge(s["w_ld"], (it // B + 1) * (16 * WDMAS))
                    pe.wait_ge(s["h_ld"], (it + 1) * 16)
                if not isinstance(it, int) or it:
                    pe.wait_ge(s["am_ok"], it * 4 - 1 + n)
                for a in range(PAIRS):
                    last = project((A0, A1)[n], a * T, lambda k: wqk[:, k, 2 * n + a, :], m)
                last.then_inc(s["qk_ps"], 1)

            def v_(st, n):
                it, m = st
                pe.wait_ge(s["tap"], it * NT * 3 + PAIRS * 3 * (n + 1))
                for j, t in enumerate((range(2), range(2, VT))[n]):
                    last = project((A0, A1)[n], j * T, lambda k: wv[:, k, t * P:(t + 1) * P], m)
                last.then_inc(s["v_ps"], 1)

            def norms(st):
                it, m = st
                pe.wait_ge(s["tap"], it * NT * 3 + 2 * PAIRS * 3)
                pe.wait_ge(s["sq_ok"], (it + 1) * 2 * PAIRS)
                for c in range(CH):
                    for n in range(2):
                        for a in range(PAIRS):
                            at = c * 2 * QH + n * QH + 2 * a
                            last = pe.matmul(ps[:, A1, T + at:T + at + 2], sq[:, n, a, c * P:(c + 1) * P],
                                             const[:, C_HEAD:C_HEAD + 2], start=True, stop=True)
                last.then_inc(s["n_ps"], 1)

            def gate(st, c):
                it, m = st
                pe.wait_ge(*((s["tap"], it * NT * 3 + (2 * PAIRS + 2) * 3), (s["gs_ok"], it * CH + 1))[c])
                for k in range(KT):
                    last = pe.matmul(ps[:, A0, 0:QV], hb[:, m, k, c * P:(c + 1) * P], wg[:, k, :],
                                     start=(k == 0), stop=(k == KT - 1))
                last.then_inc(s["g_ps"], 1)

            def keys(st):
                it, m = st
                pe.wait_ge(s["tap"], (it + 1) * NT * 3)
                pe.wait_ge(s["rk"], it + 1)
                for a in range(PAIRS):
                    last = pe.transpose(ps[:, A1, a * P:(a + 1) * P], qk[:, a, 0, 0, :], ident)
                last.then_inc(s["kt_ps"], 1)

            def scores(st, c):
                it, m = st
                for side in range(2):
                    if c == 0:
                        pe.wait_ge(*((s["gs_ok"], it * CH + 2), (s["kg_ok"], it + 1))[side])
                    else:
                        pe.wait_ge(s["am_ok"], it * 4 + side + 1)
                for a in range(PAIRS):
                    for side in range(2):
                        lo = 64 * side
                        last = pe.matmul(ps[:, (A0, A1)[side], a * 2 * P:(a + 1) * 2 * P], qk[lo:lo + 64, a, c, 0, :],
                                         qk[lo:lo + 64, a, c, :, :].rearrange("p n t -> p (n t)"), start=True, stop=True)
                last.then_inc(s["kk_ps"], 1)

            def values(st, c):
                it, m = st
                if c == 0:
                    pe.wait_ge(s["v_ok"], (it + 1) * VT)
                wait(pe, s["rs_ok"], (it - 1) * 2 * REFINE)
                wait(pe, s["r_ok"], it * CH + c if c else 0)
                for t in range(VT):
                    last = pe.transpose(ps[:, CX, t * P:(t + 1) * P], vT[:, t, c * P:(c + 1) * P], ident)
                last.then_inc(s["vt_ps"], 1)

            def heads(bank, wt, x, start):
                for h in range(QH):
                    last = pe.matmul(ps[:, bank, h * DV:(h + 1) * DV], wt(h), x[:, h * DV:(h + 1) * DV],
                                     start=(start and h == 0), stop=(h == QH - 1), skip_group_check=True)
                return last

            def w0(st, c):
                it, m = st
                pe.wait_ge(s["tt_ok"], ((it + 1) * LEVELS - 1) * 2 + c + 1)
                pe.wait_ge(s["r16_ok"], it + 1) if c == 0 else pe.wait_ge(s["r1h_ok"], it + 1)
                heads(CW, lambda h: tf[:, m, c * QH + h, :], rhs16[:, m, c, :], True).then_inc(s["w0_ps"], 1)

            def residual(st, c, r):
                it, m = st
                pe.wait_ge(s["w_ok"], (it * 2 + c) * (REFINE + 1) + r + 1)
                if c == 0 and r == 0:
                    pe.wait_ge(s["r_ok"], (it + 2) * CH if not isinstance(it, int) else min(it + 2, STEPS) * CH)
                if c == 1 and r == 0:
                    pe.wait_ge(s["r1_ok"], it + 1)
                pe.wait_ge(s["ia_ok"], it * CH + c + 1)
                heads(CX, lambda h: am[:, m, c * QH + h, 0, :], w[:, c, :], True).then_inc(s["res_ps"], 1)

            def delta(st, c, r):
                it, m = st
                pe.wait_ge(s["rs_ok"], (it * 2 + c) * REFINE + r + 1)
                heads(CW, lambda h: tf[:, m, c * QH + h, :], r16, False).then_inc(s["d_ps"], 1)

            def outputs(st, c):
                it, m = st
                pe.wait_ge(s["w_ok"], (it * 2 + c + 1) * (REFINE + 1))
                pe.wait_ge(s["acc_ok"], it * CH + c + 1)
                if c == 1:
                    for a in range(PAIRS):
                        pe.matmul(ps[:, CO, a * 2 * DV:(a + 1) * 2 * DV], kqb[:, m, a, 1, :], S[:, a, :],
                                  start=(a == 0), stop=False, skip_group_check=True)
                heads(CO, lambda h: am[:, m, c * QH + h, 1, :], w[:, c, :], c == 0).then_inc(s["o_ps"], 1)

            def state_out(st):
                it, m = st
                pe.wait_ge(s["w_ok"], (it * 2 + 1) * (REFINE + 1))
                pe.wait_ge(s["rs_ok"], (it * 2 + 1) * REFINE)
                for h in range(QH):
                    lo, at = 64 * (h % 2), (h // 2) * 2 * DV + (h % 2) * DV
                    last = pe.matmul(ps[lo:lo + 64, CX, at:at + DV], kg[:, m, h, :], w[:, 0, h * DV:(h + 1) * DV],
                                     start=True, stop=True, skip_group_check=True)
                last.then_inc(s["s_ps"], 1)
                outputs(st, 0)

            def ks(st):
                it, m = st
                pe.wait_ge(s["S_ok"], (it + 1) * 2)
                for a in range(PAIRS):
                    last = pe.matmul(ps[:, CX, a * 2 * DV:(a + 1) * 2 * DV], kqb[:, m, a, 0, :], S[:, a, :],
                                     start=True, stop=True)
                last.then_inc(s["ks_ps"], 1)

            def turn_out(st, c):
                it, m = st
                pe.wait_ge(s["og_ok"], (it * CH + c + 1) * QH)
                for t in range(VT):
                    last = pe.transpose(ps[:, CO, t * P:(t + 1) * P], og[:, c, t * P:(t + 1) * P], ident)
                last.then_inc(s["ot_ps"], 1)

            def wo_(st, c):
                it, m = st
                pe.wait_ge(s["oT_ok"], (it * CH + c + 1) * VT)
                for t in range(VT):
                    last = pe.matmul(ps[:, CO, 0:D], oT[:, t, :], wo[:, (it // B) * VT + t, :],
                                     start=(t == 0), stop=(t == VT - 1))
                last.then_inc(s["wo_ps"], 1)

            on.update(merge1=merge1, merge2=merge2, qk=qk_, v=v_, norms=norms, gate=gate, keys=keys, scores=scores,
                      values=values, w0=w0, residual=residual, delta=delta, out=outputs, state_out=state_out, ks=ks,
                      oT=turn_out, wo=wo_)
            pe.wait_ge(s["c_ld"], 32)
            run(pe, on)

        @block.vector
        def _(v):
            on = {n: nothing for n in PIECES}

            def merge1(st, l, g):
                it, m = st
                pe_done = (it * LEVELS + l) * 2 + g + 1
                v.wait_ge(s["p1"], pe_done)
                wait(v, s["p3"], pe_done - 2 if not isinstance(pe_done, int) or pe_done > 2 else 0)
                us = slice(QH * g, QH * g + QH)
                v.tensor_tensor((tn if l == 0 else w16)[:, us, :], ps[:, (X0, X1)[g], :].rearrange("p (u n) -> p u n", u=QH),
                                bc(mask[:, l, :], 1, QH), ALU.mult).then_inc(s["mask_ok"], 1)

            def taps(st, n, part):
                it, m = st
                base, tiles = 2 * n, range(2 * n, min(2 * n + 2, NT))
                order = [(x, t) for x in range(1, TAPS) for t in tiles]
                for x, t in (order[3 * part:3 * part + 3]):
                    if x == 1:
                        v.wait_ge(s["tap0"], it * NT + base + len(tiles))
                    else:
                        v.wait_ge(s["tap"], it * NT * 3 + base * 3 + (x - 2) * len(tiles) + t - base + 1)
                    off, slot = (t - base) * T, t % (2 * PAIRS)
                    v.scalar_tensor_tensor(y[:, slot, x:T], ps[:, (A0, A1)[n % 2], off:off + T - x],
                                           cw[:, t, TAPS - 1 - x:TAPS - x], y[:, slot, x:T],
                                           ALU.mult, ALU.add).then_inc(s["tap"], 1)

            def decays(st, c):
                it, m = st
                v.wait_ge(s["a_ld"], (it + 1) * 16)
                for h in range(QH):
                    u = c * QH + h
                    v.tensor_tensor_scan(dec[:, u, :], abc[:, m, h, c * P:(c + 1) * P], ident, 0.0,
                                         ALU.mult, ALU.add).then_inc(s["dec_ok"], 1)

            def gains(st):
                it, m = st
                v.wait_ge(s["n_ps"], it + 1)
                v.wait_ge(s["tap0"], (it + 1) * NT)
                n4 = ps[:, A1, T:T + 2 * U].rearrange("p (c n h) -> p c n h", c=CH, n=2)
                v.tensor_scalar(kk[:].rearrange("p (c h) -> p c h", c=CH), n4[:, :, 0, :], L2_EPS, None,
                                ALU.add).then_inc(s["nk"], 1)
                v.tensor_scalar(e2[:, m].rearrange("p (c h) -> p c h", c=CH), n4[:, :, 1, :], L2_EPS, DK * RMS_EPS,
                                ALU.add, ALU.mult).then_inc(s["rk"], 1)
                v.wait_ge(s["nk"], it + 1)
                v.reciprocal(rkk[:], kk[:]).then_inc(s["e2_ok"], 1)
                v.wait_ge(s["e2_ok"], it + 1)
                v.tensor_tensor(gam[:, m], rkk[:], mem["beta"][:, it, :], ALU.mult).then_inc(s["gam_ok"], 1)

            def keys(st):
                it, m = st
                v.wait_ge(s["gam_ok"], it + 1)
                v.wait_ge(s["dec_ok"], it * U + QH)
                v.tensor_tensor(cj[:], gam[:, m, 0:QH], dec[:, 0:QH, P - 1], ALU.mult).then_inc(s["cj_ok"], 1)
                v.wait_ge(s["cj_ok"], it + 1)
                v.wait_ge(s["kt_ps"], it + 1)
                v.tensor_tensor(kg[:, m], ps[:, A1, 0:QH * 64].rearrange("p (h d) -> p h d", h=QH),
                                bc(cj[:], 2, 64), ALU.mult).then_inc(s["kg_ok"], 1)

            def decayed(st, c, side):
                it, m = st
                v.wait_ge(s["dec_ok"], it * U + QH * (c + 1))
                v.wait_ge(s["kk_ps"], it * CH + c + 1)
                for a in range(PAIRS):
                    u = c * QH + 2 * a + side
                    ins = v.scalar_tensor_tensor(
                        am[:, m, u], ps[:, (A0, A1)[side], a * 2 * P:(a + 1) * 2 * P].rearrange("p (n t) -> p n t", n=2),
                        gam[:, m, u:u + 1], bc(dec[:, u, :], 1, 2), ALU.mult, ALU.mult)
                ins.then_inc(s["am_ok"], 1)

            def values(st, c):
                it, m = st
                v.wait_ge(s["vt_ps"], it * CH + c + 1)
                v.wait_ge(s["nrm_ok"], it + 1)
                v.tensor_tensor(rhs[:, m, c].rearrange("p (h d) -> p h d", h=QH),
                                ps[:, CX, 0:QV].rearrange("p (h d) -> p h d", h=QH),
                                bc(nrm[:, m, c * QH:(c + 1) * QH], 2, DV), ALU.mult).then_inc(s["r_ok"], 1)

            def residual(st, c, r):
                it, m = st
                v.wait_ge(s["res_ps"], (it * 2 + c) * REFINE + r + 1)
                v.tensor_tensor(r16[:], rhs[:, m, c], ps[:, CX, 0:QV], ALU.subtract).then_inc(s["rs_ok"], 1)

            def state(st):
                it, m = st
                v.wait_ge(s["s_ps"], it + 1)
                for side in range(2):
                    lo = 64 * side
                    v.tensor_copy(S[lo:lo + 64, :, side * DV:(side + 1) * DV],
                                  ps[lo:lo + 64, CX, 0:QV].rearrange("p (a n) -> p a n", a=PAIRS)[:, :, side * DV:(side + 1) * DV]
                                  ).then_inc(s["S_ok"], 1)

            def ks(st):
                it, m = st
                v.wait_ge(s["ks_ps"], it + 1)
                v.tensor_tensor(rhs[:, m, 1], rhs[:, m, 1], ps[:, CX, 0:QV], ALU.subtract).then_inc(s["r1_ok"], 1)

            def mean(st, c):
                it, m = st
                n = it * CH + c
                v.wait_ge(s["sqo_ok"], n + 1)
                v.tensor_reduce(mso[:], sqo[:].rearrange("p (h d) -> p h d", h=QH), AX_X, ALU.add).then_inc(s["mso_ok"], 1)
                v.wait_ge(s["mso_ok"], n + 1)
                v.scalar_tensor_tensor(vo[:], mso[:], 1.0 / DV, e2[:, m, c * QH:(c + 1) * QH], ALU.mult,
                                       ALU.add).then_inc(s["vo_ok"], 1)

            def gated(st, c):
                it, m = st
                v.wait_ge(s["fo_ok"], it * CH + c + 1)
                for h in range(QH):
                    hs = slice(h * DV, (h + 1) * DV)
                    v.scalar_tensor_tensor(og[:, c, hs], ps[:, CO, hs], fo[:, h:h + 1], gs[:, m, c, hs], ALU.mult,
                                           ALU.mult).then_inc(s["og_ok"], 1)

            def acc(st, c):
                it, m = st
                v.wait_ge(s["wo_ps"], it * CH + c + 1)
                at = mem["acc"][:, (it % B) * CH + c, :]
                v.tensor_tensor(at, at, ps[:, CO, 0:D], ALU.add).then_inc(s["acc_ok"], 1)

            on.update(merge1=merge1, taps=taps, decays=decays, gains=gains, keys=keys, decayed=decayed, values=values,
                      residual=residual, state_out=state, ks=ks, mean=mean, gated=gated, acc=acc)
            v.memset(wqk[:], 0.0).then_inc(s["set_ok"], 1)
            v.memset(cw[:], 0.0).then_inc(s["set_ok"], 1)
            v.memset(S[:], 0.0).then_inc(s["set_ok"], 1)
            v.memset(mso[:], 0.0).then_inc(s["acc_ok"], 1)
            v.wait_ge(s["set_ok"], 6)
            run(v, on)

        @block.scalar
        def _(act):
            on = {n: nothing for n in PIECES}

            def merge2(st, l, g):
                it, m = st
                us = slice(QH * g, QH * g + QH)
                if 0 < l < LEVELS - 1:
                    act.wait_ge(s["p2"], (it * (LEVELS - 2) + l - 1) * 2 + g + 1)
                    act.copy(tn[:, us, :], ps[:, (X2, X1)[g], :].rearrange("p (u n) -> p u n", u=QH)).then_inc(s["tn_ok"], 1)
                act.wait_ge(s["p3"], (it * LEVELS + l) * 2 + g + 1)
                dst = tf[:, m, us, :] if l == LEVELS - 1 else tt[:, us, :]
                act.copy(dst, ps[:, (X0, X2)[g], :].rearrange("p (u n) -> p u n", u=QH)).then_inc(s["tt_ok"], 1)

            def qk_(st, n):
                it, m = st
                act.wait_ge(s["qk_ps"], it * 2 + n + 1)
                wait(act, s["v_ok"], it * VT)
                for a in range(PAIRS):
                    act.activation(y[:, 2 * n + a, :], ps[:, (A0, A1)[n], a * T:(a + 1) * T], ACT.Copy,
                                   scale=cw[:, 2 * n + a, TAPS - 1:TAPS]).then_inc(s["tap0"], 1)

            def qk_silu(st, n):
                it, m = st
                wait(act, s["kk_ps"], it * CH)
                wait(act, s["kqb_ok"], it * PAIRS)
                for a in range(PAIRS):
                    act.wait_ge(s["tap"], it * NT * 3 + n * PAIRS * 3 + 2 * PAIRS + a + 1)
                    act.activation(qk[:, a, :, 1 - n, :], y[:, 2 * n + a, :].rearrange("p (c t) -> p c t", c=CH),
                                   ACT.Silu).then_inc(s["qk_ok"], 1)
                act.wait_ge(s["qk_ok"], it * 2 * PAIRS + (n + 1) * PAIRS)
                wait(act, s["n_ps"], it)
                act.activation(sq[:, 1 - n, 1, :].rearrange("p (c t) -> p c t", c=CH), qk[:, 1, :, 1 - n, :],
                               ACT.Square).then_inc(s["sq_ok"], 1)

            def v_(st, n):
                it, m = st
                act.wait_ge(s["v_ps"], it * 2 + n + 1)
                act.wait_ge(s["qk_ok"], it * 2 * PAIRS + (n + 1) * PAIRS)
                for j, t in enumerate((range(2), range(2, VT))[n]):
                    act.activation(y[:, t, :], ps[:, (A0, A1)[n], j * T:(j + 1) * T], ACT.Copy,
                                   scale=cw[:, 2 * PAIRS + t, TAPS - 1:TAPS]).then_inc(s["tap0"], 1)

            def v_silu(st, n):
                it, m = st
                wait(act, s["vt_ps"], it * CH)
                tiles = (range(2), range(2, VT))[n]
                for j, t in enumerate(tiles):
                    act.wait_ge(s["tap"], it * NT * 3 + (2 * PAIRS + 2 * n) * 3 + 2 * len(tiles) + j + 1)
                    act.activation(vT[:, t, :], y[:, t, :], ACT.Silu).then_inc(s["v_ok"], 1)

            def gate(st, c):
                it, m = st
                act.wait_ge(s["g_ps"], it * CH + c + 1)
                wait(act, s["og_ok"], (it - NB + 1) * CH * QH)
                act.activation(gs[:, m, c, :], ps[:, A0, 0:QV], ACT.Silu).then_inc(s["gs_ok"], 1)

            def negate(st, c):
                it, m = st
                act.wait_ge(s["am_ok"], it * 4 + 2 * c + 2)
                act.activation(b16[:, m, c * QH:(c + 1) * QH, :], am[:, m, c * QH:(c + 1) * QH, 0, :], ACT.Copy,
                               scale=-1.0).then_inc(s["b16_c"], 1)

            def round_(st, c):
                it, m = st
                act.wait_ge(s["r_ok"], it * CH + 1)
                act.copy(rhs16[:, m, 0, :], rhs[:, m, 0, :]).then_inc(s["r16_ok"], 1)

            def copy_w(it, c, n):
                k = (it * 2 + c) * (REFINE + 1) + n + 1
                act.copy(w[:, c, :], ps[:, CW, 0:QV]).then_inc(s["w_ok"], 1)

            def w0(st, c):
                it, m = st
                act.wait_ge(s["w0_ps"], it * CH + c + 1)
                copy_w(it, c, 0)

            def delta(st, c, r):
                it, m = st
                act.wait_ge(s["d_ps"], (it * 2 + c) * REFINE + r + 1)
                copy_w(it, c, r + 1)

            def squares(st, c):
                it, m = st
                act.wait_ge(s["o_ps"], it * CH + c + 1)
                act.activation(sqo[:], ps[:, CO, 0:QV], ACT.Square).then_inc(s["sqo_ok"], 1)

            def ks(st):
                it, m = st
                act.wait_ge(s["r1_ok"], it + 1)
                act.copy(rhs16[:, m, 1, :], rhs[:, m, 1, :]).then_inc(s["r1h_ok"], 1)

            def turn_out(st, c):
                it, m = st
                act.wait_ge(s["ot_ps"], it * CH + c + 1)
                for t in range(VT):
                    act.activation(oT[:, t, :], ps[:, CO, t * P:(t + 1) * P], ACT.Copy,
                                   scale=gw[:, t:t + 1]).then_inc(s["oT_ok"], 1)

            on.update(merge2=merge2, qk=qk_, qk_silu=qk_silu, v=v_, v_silu=v_silu, gate=gate, negate=negate, round=round_,
                      w0=w0, delta=delta, state_out=lambda st: squares(st, 0), out=squares, ks=ks, oT=turn_out)
            act.wait_ge(s["c_ld"], 32)
            run(act, on)

        @block.gpsimd
        def _(pool):
            on = {n: nothing for n in PIECES}

            def squares(st, n):
                it, m = st
                wait_apart(pool, s["n_ps"], it, s["passed_pool"])
                wait_apart(pool, s["qk_ok"], it * 2 * PAIRS + n * PAIRS + 1, s["passed_pool"])
                pool.tensor_tensor(sq[:, 1 - n, 0, :].rearrange("p (c t) -> p c t", c=CH), qk[:, 0, :, 1 - n, :],
                                   qk[:, 0, :, 1 - n, :], ALU.mult).then_inc(s["sq_ok"], 1)

            def gains(st):
                it, m = st
                wait_apart(pool, s["nk"], it + 1, s["passed_pool"])
                pool.tensor_tensor(nrm[:, m], kk[:], half[:], ALU.pow).then_inc(s["nrm_ok"], 1)
                wait_apart(pool, s["qk_ok"], (it + 1) * 2 * PAIRS, s["passed_pool"])
                wait_apart(pool, s["b_ld"], (it + 1) * 32, s["passed_pool"])
                for a in range(PAIRS):
                    pool.tensor_tensor(kqb[:, m, a], qk[:, a, 1], bc(bcb[:, m, a, :], 1, 2), ALU.mult).then_inc(s["kqb_ok"], 1)

            def select(st, c):
                it, m = st
                us = slice(c * QH, (c + 1) * QH)
                wait_apart(pool, s["b16_c"], it * CH + c + 1, s["passed_pool"])
                pool.affine_select(b16[:, m, us, :], b16[:, m, us, :], [[0, QH], [-1, P]], ALU.not_equal, 1.0, base=0,
                                   channel_multiplier=1).then_inc(s["b16_ok"], 1)
                pool.affine_select(am[:, m, us, 0, :], am[:, m, us, 0, :], [[0, QH], [-1, P]], ALU.not_equal, 1.0, base=0,
                                   channel_multiplier=1).then_inc(s["ia_ok"], 1)

            def scale(st, c):
                it, m = st
                wait_apart(pool, s["vo_ok"], it * CH + c + 1, s["passed_pool"])
                pool.tensor_tensor(fo[:], vo[:], nhalf[:], ALU.pow).then_inc(s["fo_ok"], 1)

            on.update(qk_silu=squares, gains=gains, negate=select, mean=scale)
            pool.memset(half[:], 0.5).then_inc(s["set_ok"], 1)
            pool.memset(nhalf[:], -0.5).then_inc(s["set_ok"], 1)
            pool.memset(vo[:], 1.0).then_inc(s["set_ok"], 1)
            pool.wait_ge(s["set_ok"], 6)
            run(pool, on)



def experts(nc, A, mem, scr):
    with ExitStack() as ctx:
        sb = lambda name, shape, dt=F32: ctx.enter_context(nc.sbuf_tensor("ex_" + name, shape, dt))
        sem = lambda name: ctx.enter_context(nc.semaphore("ex_" + name))
        ps = ctx.enter_context(nc.psum_tensor("ex_ps", [P, 8, 512], F32))
        W1 = sb("W1", [P, KT, INTER])
        W3 = sb("W3", [P, KT, INTER])
        W2 = sb("W2", [P, MT, D])
        w2c = sb("w2c", [P, KT])
        gate_w = sb("gate_w", [P, KT, E])
        ew1 = sb("ew1", [P, KT, E, HID])
        eb1 = sb("eb1", [P, E])
        ew2 = sb("ew2", [P, E, D])
        b2 = sb("b2", [E + 1, D])
        sw1 = sb("sw1", [P, KT, SH])
        sb1 = sb("sb1", [P, SH // P])
        sw2 = sb("sw2", [P, SH // P, D])
        modb = sb("modb", [P, 2, 4, D])
        xg = sb("xg", [P, GT, D])
        x2 = sb("x2", [P, GT, D])
        hn = sb("hn", [P, GT, D])
        sq = sb("sq", [P, GT, D])
        ss, ms, rr, nh, var, rstd = (sb(n, [P, GT]) for n in ("ss", "ms", "rr", "nh", "var", "rstd"))
        st = sb("st", [P, GT, 6])
        mv = sb("mv", [P, GT, 2])
        fT = sb("fT", [P, KT, GTOK])
        s1 = sb("s1", [P, 2, GTOK])
        gT = sb("gT", [P, MT, GTOK])
        lg = sb("lg", [P, GT, E])
        top = sb("top", [P, GT, E])
        idx = sb("idx", [P, GT, E], U32)
        idf = sb("idf", [P, GT, 2])
        dl = sb("dl", [P, GT])
        ed = sb("ed", [P, GT])
        pr = sb("pr", [P, GT, 2])
        g2 = sb("g2", [P, GT, E])
        gates = sb("gates", [P, GT, 16])
        gT9 = sb("gT9", [E + 1, GTOK])
        shT = sb("shT", [P, SH // P, GTOK])
        he = sb("he", [P, 2, GTOK])
        yo = sb("yo", [P, GT, D])

        names = """ld x_ld mod_ld out_st set_ok ss_ok ms_ok rr_ok hn_ok tr_ps fT_ok h1_ps s1_ok gT_ok o2_ps x2_ok
            var_ok rstd_ok lg_ps dl_ok ed_ok gates_ok gt_ps gt9_ok sh_ps shT_ok he_ps he_ok y0_ps y0_ok e_ps e_ok out_ok
            chain passed passed_pool passed_sp""".split()
        s = {n: sem(n) for n in names}
        const = mem["const"]
        ident = const[:, C_ID:C_ID + P]
        acc = mem["acc"]
        SLOTS = SH // P
        LDS = 15

        block = ctx.enter_context(nc.Block())

        @block.sync
        def _(sp):
            k_of = lambda ap: ap.rearrange("(k p) n -> p k n", k=KT)
            full = (INTER // P) * P
            loads = [(W1[:], k_of(A["W1"])), (W3[:], k_of(A["W3"])),
                     (W2[:, 0:MT - 1, :], A["W2"][0:full, :].rearrange("(t p) n -> p t n", p=P)),
                     (W2[0:INTER - full, MT - 1, :], A["W2"][full:INTER, :]),
                     (w2c[:], A["rms2_w"]),
                     (gate_w[:], k_of(A["gate_w"]))]
            for k in range(KT):
                loads.append((ew1[:, k], A["w1"][:, k * P:(k + 1) * P, :].rearrange("e p h -> p e h")))
            loads += [(eb1[:], A["b1"]), (ew2[:], A["w2"].rearrange("e h d -> h e d")),
                      (b2[0:E, :], A["b2"]), (b2[E:E + 1, :], A["shared_b2"].rearrange("(a d) -> a d", a=1)),
                      (sw1[:], k_of(A["shared_w1"])), (sb1[:], A["shared_b1"]),
                      (sw2[:], A["shared_w2"].rearrange("(t p) d -> p t d", p=P))]
            assert len(loads) == LDS
            for dst, src in loads:
                sp.dma_start(dst, src).then_inc(s["ld"], 16)
            x_v = A["x"].rearrange("b (c p) d -> p (b c) d", p=P)
            o_v = A["out"].rearrange("b (c p) d -> p (b c) d", p=P)
            def turn(g):
                wait_apart(sp, s["out_ok"], g, s["passed_sp"])
                sp.dma_start(modb[:], scr["mod"][bass.ds(g * 2, 2), 2 * D:6 * D].rearrange("b (n d) -> b n d", n=4)
                             .partition_broadcast(P)).then_inc(s["mod_ld"], 16)
                sp.dma_start(xg[:], x_v[:, bass.ts(g, GT), :]).then_inc(s["x_ld"], 16)
                wait_apart(sp, s["out_ok"], g + 1, s["passed_sp"])
                sp.dma_start(o_v[:, bass.ts(g, GT), :], yo[:]).then_inc(s["out_st"], 16)

            groups(sp, turn)
            sp.wait_ge(s["out_st"], 16 * GROUPS)

        @block.tensor
        def _(pe):
            pe.wait_ge(s["ld"], 16 * LDS)
            def turn(g):
                def transposes(n):
                    pe.wait_ge(s["hn_ok"], (g * 2 + n + 1) * GT)
                    for k in range(KT):
                        for j in range(GT):
                            last = pe.transpose(ps[:, k, j * P:(j + 1) * P], hn[:, j, k * P:(k + 1) * P], ident)
                        last.then_inc(s["tr_ps"], 1)
                    pe.wait_ge(s["fT_ok"], (g * 2 + n + 1) * KT)

                wait(pe, s["e_ok"], g * E * GT)
                transposes(0)
                for m in range(MT):
                    M = min(P, INTER - m * P)
                    if m >= 2:
                        pe.wait_ge(s["gT_ok"], g * MT + m - 1)
                    else:
                        wait(pe, s["he_ok"], g * E)
                    for n, wt in enumerate((W1, W3)):
                        for k in range(KT):
                            last = pe.matmul(ps[0:M, 2 + 2 * (m % 2) + n, :], wt[:, k, m * P:m * P + M], fT[:, k, :],
                                             start=(k == 0), stop=(k == KT - 1))
                        last.then_inc(s["h1_ps"], 1)
                pe.wait_ge(s["gT_ok"], (g + 1) * MT)
                wait(pe, s["y0_ok"], g)
                for j in range(GT):
                    for m in range(MT):
                        M = min(P, INTER - m * P)
                        last = pe.matmul(ps[:, 6 + j // 2, (j % 2) * D:(j % 2 + 1) * D], gT[0:M, m, j * P:(j + 1) * P],
                                         W2[0:M, m, :], start=(m == 0), stop=(m == MT - 1))
                    if j % 2:
                        last.then_inc(s["o2_ps"], 1)
                transposes(1)
                for j in range(GT):
                    for k in range(KT):
                        last = pe.matmul(ps[:, 2, j * E:(j + 1) * E], fT[:, k, j * P:(j + 1) * P], gate_w[:, k, :],
                                         start=(k == 0), stop=(k == KT - 1))
                last.then_inc(s["lg_ps"], 1)
                for n in range(SLOTS):
                    for k in range(KT):
                        last = pe.matmul(ps[:, 4 + n, :], sw1[:, k, n * P:(n + 1) * P], fT[:, k, :],
                                         start=(k == 0), stop=(k == KT - 1))
                    last.then_inc(s["sh_ps"], 1)
                pe.wait_ge(s["gates_ok"], g + 1)
                for j in range(GT):
                    last = pe.transpose(ps[0:E + 1, 3, j * P:(j + 1) * P], gates[:, j, 0:E + 1], ident)
                last.then_inc(s["gt_ps"], 1)

                def hidden(e):
                    if e < 2:
                        pe.wait_ge(s["shT_ok"], g * SLOTS + e + 1)
                    else:
                        pe.wait_ge(s["he_ok"], g * E + e - 1)
                    for k in range(KT):
                        last = pe.matmul(ps[:, 4 + e % 2, :], ew1[:, k, e, :], fT[:, k, :], start=(k == 0),
                                         stop=(k == KT - 1))
                    last.then_inc(s["he_ps"], 1)

                hidden(0)
                pe.wait_ge(s["shT_ok"], (g + 1) * SLOTS)
                pe.wait_ge(s["gt9_ok"], g + 1)
                pe.wait_ge(s["x2_ok"], (g + 1) * 2)
                for j in range(GT):
                    out = ps[:, 6 + j // 2, (j % 2) * D:(j % 2 + 1) * D]
                    for n in range(SLOTS):
                        pe.matmul(out, shT[:, n, j * P:(j + 1) * P], sw2[:, n, :], start=(n == 0), stop=False)
                    last = pe.matmul(out, gT9[:, j * P:(j + 1) * P], b2[:], start=False, stop=True)
                last.then_inc(s["y0_ps"], 1)
                for e in range(E):
                    if e + 1 < E:
                        hidden(e + 1)
                    pe.wait_ge(s["he_ok"], g * E + e + 1)
                    if e >= 2:
                        pe.wait_ge(s["e_ok"], (g * E + e - 1) * GT)
                    for j in range(GT):
                        last = pe.matmul(ps[:, 2 * (e % 2) + j // 2, (j % 2) * D:(j % 2 + 1) * D],
                                         he[:, e % 2, j * P:(j + 1) * P], ew2[:, e, :], start=True, stop=True)
                    last.then_inc(s["e_ps"], 1)

            groups(pe, turn)

        @block.gpsimd
        def _(pool):
            pool.memset(nh[:], -0.5).then_inc(s["set_ok"], 1)
            pool.wait_ge(s["set_ok"], 1)
            def turn(g):
                wait_apart(pool, s["ms_ok"], g + 1, s["passed_pool"])
                pool.tensor_tensor(rr[:], ms[:], nh[:], ALU.pow).then_inc(s["rr_ok"], 1)
                for n in range(2):
                    wait_apart(pool, s["var_ok"], g * 2 + n + 1, s["passed_pool"])
                    pool.tensor_tensor(rstd[:, 2 * n:2 * n + 2], var[:, 2 * n:2 * n + 2], nh[:, 2 * n:2 * n + 2],
                                       ALU.pow).then_inc(s["rstd_ok"], 1)

            groups(pool, turn)

        @block.scalar
        def _(act):
            act.wait_ge(s["ld"], 16 * LDS)
            def turn(g):
                wait(act, s["ms_ok"], g)
                for j in range(GT):
                    act.activation(sq[:, j, :], acc[:, g * GT + j, :], ACT.Square, accum_out=ss[:, j:j + 1]).then_inc(s["ss_ok"], 1)
                for k in range(KT):
                    act.wait_ge(s["tr_ps"], g * 2 * KT + k + 1)
                    act.activation(fT[:, k, :], ps[:, k, :], ACT.Copy, scale=w2c[:, k:k + 1]).then_inc(s["fT_ok"], 1)
                for m in range(MT):
                    M = min(P, INTER - m * P)
                    act.wait_ge(s["h1_ps"], (g * MT + m) * 2 + 1)
                    if m >= 2:
                        act.wait_ge(s["gT_ok"], g * MT + m - 1)
                    act.activation(s1[0:M, m % 2, :], ps[0:M, 2 + 2 * (m % 2), :], ACT.Silu).then_inc(s["s1_ok"], 1)
                for k in range(KT):
                    act.wait_ge(s["tr_ps"], g * 2 * KT + KT + k + 1)
                    act.copy(fT[:, k, :], ps[:, k, :]).then_inc(s["fT_ok"], 1)
                act.wait_ge(s["dl_ok"], g + 1)
                act.activation(ed[:], dl[:], ACT.Exp).then_inc(s["ed_ok"], 1)
                for n in range(SLOTS):
                    act.wait_ge(s["sh_ps"], g * SLOTS + n + 1)
                    act.activation(shT[:, n, :], ps[:, 4 + n, :], ACT.Gelu, bias=sb1[:, n:n + 1]).then_inc(s["shT_ok"], 1)
                act.wait_ge(s["gt_ps"], g + 1)
                act.copy(gT9[:], ps[0:E + 1, 3, :]).then_inc(s["gt9_ok"], 1)
                for e in range(E):
                    act.wait_ge(s["he_ps"], g * E + e + 1)
                    if e >= 2:
                        act.wait_ge(s["e_ps"], g * E + e - 1)
                    act.activation(he[:, e % 2, :], ps[:, 4 + e % 2, :], ACT.Gelu, bias=eb1[:, e:e + 1]).then_inc(s["he_ok"], 1)

            groups(act, turn)

        @block.vector
        def _(v):
            v.memset(gates[:], 1.0)
            def turn(g):
                c = Chain(v, s["chain"], g, CHAIN_EX)
                v.wait_ge(s["ss_ok"], (g + 1) * GT)
                v.tensor_scalar(ms[:], ss[:], 1.0 / D, RMS_EPS, ALU.mult, ALU.add).then_inc(s["ms_ok"], 1)
                v.wait_ge(s["rr_ok"], g + 1)
                for j in range(GT):
                    v.tensor_scalar(hn[:, j, :], acc[:, g * GT + j, :], rr[:, j:j + 1], None, ALU.mult).then_inc(s["hn_ok"], 1)
                for m in range(MT):
                    M = min(P, INTER - m * P)
                    v.wait_ge(s["s1_ok"], g * MT + m + 1)
                    v.wait_ge(s["h1_ps"], (g * MT + m) * 2 + 2)
                    v.tensor_tensor(gT[0:M, m, :], s1[0:M, m % 2, :], ps[0:M, 3 + 2 * (m % 2), :], ALU.mult).then_inc(s["gT_ok"], 1)
                for n in range(2):
                    js = range(2 * n, 2 * n + 2)
                    v2 = x2[:, 2 * n:2 * n + 2, :]
                    v.wait_ge(s["o2_ps"], g * 2 + n + 1)
                    c.link(v.tensor_tensor(v2, acc[:, bass.ds(g * GT + 2 * n, 2), :],
                                           ps[:, 6 + n, :].rearrange("p (j d) -> p j d", j=2), ALU.add))
                    v.wait_ge(s["mod_ld"], (g + 1) * 16)
                    c.link(v.tensor_tensor(v2, v2, bc(modb[:, n, 0, :], 1, 2), ALU.mult))
                    v.wait_ge(s["x_ld"], (g + 1) * 16)
                    v.tensor_tensor(v2, v2, xg[:, 2 * n:2 * n + 2, :], ALU.add).then_inc(s["x2_ok"], 1)
                    v.wait_ge(s["x2_ok"], g * 2 + n + 1)
                    for j in js:
                        c.add(v.bn_stats(st[:, j, :], x2[:, j, :]))
                    c.sync_apart(s["passed"])
                    for j in js:
                        c.add(v.bn_aggr(mv[:, j, :], st[:, j, :]))
                    c.sync()
                    v.tensor_scalar(var[:, 2 * n:2 * n + 2], mv[:, 2 * n:2 * n + 2, 1], RMS_EPS, None,
                                    ALU.add).then_inc(s["var_ok"], 1)
                    v.wait_ge(s["rstd_ok"], g * 2 + n + 1)
                    for j in js:
                        c.add(v.tensor_scalar(hn[:, j, :], x2[:, j, :], mv[:, j, 0:1], rstd[:, j:j + 1], ALU.subtract,
                                              ALU.mult))
                    c.sync()
                    v2 = hn[:, 2 * n:2 * n + 2, :]
                    c.link(v.tensor_tensor(v2, v2, bc(modb[:, n, 2, :], 1, 2), ALU.mult))
                    v.tensor_tensor(v2, v2, bc(modb[:, n, 1, :], 1, 2), ALU.add).then_inc(s["hn_ok"], 2)
                v.wait_ge(s["lg_ps"], g + 1)
                c.add(v.tensor_copy(lg[:], ps[:, 2, 0:GT * E].rearrange("p (j e) -> p j e", j=GT)))
                c.sync_apart(s["passed"])
                for j in range(GT):
                    c.add(v.max(top[:, j, :], lg[:, j, :]))
                c.sync()
                v.tensor_tensor(dl[:], top[:, :, 1], top[:, :, 0], ALU.subtract).then_inc(s["dl_ok"], 1)
                for j in range(GT):
                    c.add(v.max_index(idx[:, j, :], top[:, j, :], lg[:, j, :]))
                c.sync()
                c.link(v.tensor_copy(idf[:], idx[:, :, 0:2]))
                v.wait_ge(s["ed_ok"], g + 1)
                c.link(v.tensor_scalar(dl[:], ed[:], 1.0, None, ALU.add))
                c.link(v.reciprocal(pr[:, :, 0], dl[:]))
                c.link(v.tensor_tensor(pr[:, :, 1], pr[:, :, 0], ed[:], ALU.mult))
                for j in range(GT):
                    for n, dst in ((0, gates[:, j, 0:E]), (1, g2[:, j, :])):
                        c.add(v.tensor_scalar(dst, const[:, C_IOTA:C_IOTA + E], idf[:, j, n:n + 1], pr[:, j, n:n + 1],
                                              ALU.is_equal, ALU.mult))
                c.sync()
                v.tensor_tensor(gates[:, :, 0:E], gates[:, :, 0:E], g2[:], ALU.add).then_inc(s["gates_ok"], 1)
                v.wait_ge(s["y0_ps"], g + 1)
                wait(v, s["out_st"], g * 16)
                v.tensor_copy(yo[:].rearrange("p (n j) d -> p n (j d)", n=2), ps[:, 6:8, :]).then_inc(s["y0_ok"], 1)
                v.wait_ge(s["y0_ok"], g + 1)
                for e in range(E):
                    v.wait_ge(s["e_ps"], g * E + e + 1)
                    if e:
                        v.wait_ge(s["e_ok"], (g * E + e) * GT)
                    for j in range(GT):
                        v.scalar_tensor_tensor(yo[:, j, :], ps[:, 2 * (e % 2) + j // 2, (j % 2) * D:(j % 2 + 1) * D],
                                               gates[:, j, e:e + 1], yo[:, j, :], ALU.mult, ALU.add).then_inc(s["e_ok"], 1)
                v.wait_ge(s["e_ok"], (g + 1) * E * GT)
                for n in range(2):
                    v2 = yo[:, 2 * n:2 * n + 2, :]
                    c.add(v.tensor_tensor(v2, v2, bc(modb[:, n, 3, :], 1, 2), ALU.mult))
                c.sync()
                v.tensor_tensor(yo[:], yo[:], x2[:], ALU.add).then_inc(s["out_ok"], 1)
                c.close()

            groups(v, turn)


CHAIN_EX = 41


def adaln_block(nc, A):
    with ExitStack() as ctx:
        sb = lambda name, shape, dt=F32: ctx.enter_context(nc.sbuf_tensor(name, shape, dt))
        mem = {
            "const": sb("const", [P, C_COLS]),
            "id16": sb("id16", [P, P], BF16),
            "mask": sb("mask", [P, LEVELS, P], BF16),
            "acc": sb("acc", [P, TILES, D]),
            "hT": sb("hT", [P, KT, B * T]),
            "beta": sb("beta", [P, STEPS, U]),
        }
        scr = {
            "mod": nc.dram_tensor("scr_mod", (B, 6 * D), F32, kind="Internal").ap(),
            "a": nc.dram_tensor("scr_a", (B, H, T), F32, kind="Internal").ap(),
            "b": nc.dram_tensor("scr_b", (B, H, P), F32, kind="Internal").ap(),
        }
        prepare(nc, A, mem, scr)
        delta_rule(nc, A, mem, scr)
        experts(nc, A, mem, scr)


def constants():
    import numpy as np

    c = np.zeros((P, C_COLS), np.float32)
    i = np.arange(P)
    c[:, C_ID:C_ID + P] = np.eye(P)
    for l in range(LEVELS):
        size = 1 << l
        same = i[:, None] // (2 * size) == i[None, :] // (2 * size)
        other = i[:, None] // size != i[None, :] // size
        c[:, C_MASK + l * P:C_MASK + (l + 1) * P] = (same & other) | (i[:, None] == i[None, :])
    c[0:64, C_HEAD] = 1.0
    c[64:128, C_HEAD + 1] = 1.0
    c[:, C_IOTA:C_IOTA + E] = np.arange(E)
    return c


_ATTN = ["x", "rms1_w", "rms2_w", "Wq", "Wk", "Wv", "Wa", "Wb", "Wg", "dt_bias", "A_log", "conv_q_w", "conv_k_w",
         "conv_v_w", "gnorm_w", "Wo", "W1", "W3", "W2"]
_FFN = ["gate_w", "w1", "b1", "w2", "b2", "shared_w1", "shared_b1", "shared_w2", "shared_b2"]


def kernel(**inputs):
    import numpy as np
    import concourse.bacc as bacc
    from concourse.bass_utils import run_bass_kernel_spmd

    nc = bacc.Bacc("TRN2", target_bir_lowering=False, num_devices=1)
    named = {n: "L0_attn_" + n for n in _ATTN} | {n: "L0_ffn_" + n for n in _FFN} | {"c": "L0_c", "wmod": "L0_wmod"}
    host = {n: np.asarray(inputs[full]) for n, full in named.items()}
    host["c"] = host["c"].T.reshape(KT, P, B).transpose(1, 0, 2)
    host["b1"] = host["b1"].T
    for n in ("rms1_w", "rms2_w", "shared_b1"):
        host[n] = host[n].reshape(-1, P).T
    host["gnorm_w"] = np.concatenate([host["gnorm_w"]] * QH).reshape(VT, P).T
    host = {n: np.ascontiguousarray(a) for n, a in host.items()}
    host["consts"] = constants()
    A = {n: nc.dram_tensor("in_" + n, a.shape, mybir.dt.from_np(a.dtype), kind="ExternalInput").ap()
         for n, a in host.items()}
    A["out"] = nc.dram_tensor("out", (B, T, D), F32, kind="ExternalOutput").ap()
    adaln_block(nc, A)
    r = run_bass_kernel_spmd(nc, [{"in_" + n: a for n, a in host.items()}], core_ids=[0])
    return r.results[0]["out"]
```
